# Optimizing a Trainium2 kernel written in Bass

```python
import numpy as np
import jax
import jax.numpy as jnp

def _softmax(x, axis=-1):
    return jax.nn.softmax(x, axis=axis)

def _gelu(x):
    return jax.nn.gelu(x, approximate=True)

def _silu(x):
    return jax.nn.silu(x)

def _sigmoid(x):
    return jax.nn.sigmoid(x)

def _layernorm(x, axis=-1, eps=1e-05):
    m = jnp.mean(x, axis=axis, keepdims=True)
    v = jnp.var(x, axis=axis, keepdims=True)
    return (x - m) / jnp.sqrt(v + eps)

def _scatter_add(tgt, idx, src, axis=0):
    return tgt.at[idx].add(src)

def _segment_sum(src, seg, n):
    return jax.ops.segment_sum(src, seg, n)
kernel_name = 'mk_decoder_postln_d2_seqx_r8_251ece'

def setup_inputs(seed: int=0):
    np.random.seed(seed)
    _w = jnp.asarray

    def _rec_inputs():
        import jax
        import jax.numpy as jnp
        _rk = jax.random.key(seed)
        x = -0.0002928 + 1 * jax.random.normal(jax.random.fold_in(_rk, 1), (32, 128, 128), jnp.float32)
        _lenS = 128 - jax.random.randint(jax.random.fold_in(_rk, 7), (32,), 0, max(1, 128 // 4) + 1, jnp.int32)
        _lenS2 = 128 - jax.random.randint(jax.random.fold_in(_rk, 8), (32,), 0, max(1, 128 // 4) + 1, jnp.int32)
        _ctx_1024P = jax.random.normal(jax.random.fold_in(_rk, 11), (32, 16, 128), jnp.float32)
        _ctx_1024c = jax.random.dirichlet(jax.random.fold_in(_rk, 511), 0.3 * jnp.ones((16,), jnp.float32), (32, 128))
        _ctx_1024t = jnp.einsum('bsk,bkd->bsd', _ctx_1024c, _ctx_1024P)
        _ctx_1024t = _ctx_1024t * jax.lax.rsqrt(jnp.mean(jnp.square(_ctx_1024t)) + 1e-12) * 0.953939
        ctx_1024 = -1.39393e-06 + 0.999914 * (_ctx_1024t + 0.3 * jax.random.normal(jax.random.fold_in(_rk, 611), (32, 128, 128), jnp.float32))
        _validS = jnp.arange(128)[None, :] < _lenS[:, None]
        _validS2 = jnp.arange(128)[None, :] < _lenS2[:, None]
        _causal = jnp.tril(jnp.ones((128, 128), dtype=bool))
        mask_Bx1xSxS2_ik1 = jnp.where(jnp.broadcast_to(_validS2[:, None, None, :], (32, 1, 128, 128)), 1, 0).astype(jnp.int32)
        return (x, ctx_1024, mask_Bx1xSxS2_ik1)
    x, ctx_1024, mask_Bx1xSxS2_ik1 = _rec_inputs()

    def _L0_attn_setup():
        import jax, jax.numpy as jnp
        import numpy as np
        B, N, DIM = (4, 512, 128)
        H, M = (16, 64)
        HD = DIM // H

        def iterative_inv(mat, n_iter=6):
            m = mat.shape[-1]
            I = jnp.eye(m, dtype=mat.dtype)
            K = mat
            denom = jnp.max(jnp.sum(K, axis=-2), axis=-1)[:, :, None, None]
            V = jnp.swapaxes(K, -1, -2) / denom
            for _ in range(n_iter):
                KV = jnp.matmul(K, V)
                V = jnp.matmul(0.25 * V, 13 * I - jnp.matmul(KV, 15 * I - jnp.matmul(KV, 7 * I - KV)))
            return V

        def _reference_tuple_inner(x, w_qkv, w_proj):
            b, n, c = x.shape
            qkv = (x @ w_qkv).reshape(b, n, 3, H, HD)
            qkv = jnp.transpose(qkv, (2, 0, 3, 1, 4))
            Q, K, V = (qkv[0], qkv[1], qkv[2])
            Q = Q / jnp.asarray(HD ** 0.5, dtype=Q.dtype)
            Q_l = Q.reshape(b, H, M, n // M, HD).mean(axis=-2)
            K_l = K.reshape(b, H, M, n // M, HD).mean(axis=-2)
            kernel1 = jax.nn.softmax(jnp.einsum('bhnd,bhmd->bhnm', Q, K_l), axis=-1)
            kernel2 = jax.nn.softmax(jnp.einsum('bhmd,bhkd->bhmk', Q_l, K_l), axis=-1)
            kernel3 = jax.nn.softmax(jnp.einsum('bhmd,bhnd->bhmn', Q_l, K), axis=-1)
            SV = jnp.matmul(jnp.matmul(kernel1, iterative_inv(kernel2)), jnp.matmul(kernel3, V))
            SV = jnp.transpose(SV, (0, 2, 1, 3)).reshape(b, n, c)
            out = SV @ w_proj
            return (out, SV)
        key = jax.random.key(seed)
        k1, k2, k3 = jax.random.split(key, 3)
        x = jax.random.normal(k1, (B, N, DIM), dtype=jnp.float32)
        w_qkv = jax.random.normal(k2, (DIM, 3 * DIM), dtype=jnp.float32) * 0.02
        w_proj = jax.random.normal(k3, (DIM, DIM), dtype=jnp.float32) * 0.02
        return {'x': x, 'w_qkv': w_qkv, 'w_proj': w_proj}
    _L0_attn_all = _L0_attn_setup()
    _L0_attn_in = {k: v for k, v in _L0_attn_all.items() if k in ('w_qkv', 'w_proj')}
    del _L0_attn_all

    def _L0_xattn_setup():
        import jax, jax.numpy as jnp
        import numpy as np
        EMBED_DIM = 128
        NUM_HEADS = 16
        HEAD_DIM = EMBED_DIM // NUM_HEADS
        SCALE = HEAD_DIM ** (-0.5)
        key = jax.random.key(seed)
        k1, k2, k3, k4, k5, k6 = jax.random.split(key, 6)
        B, Tq, Tk = (2, 256, 256)
        std = EMBED_DIM ** (-0.5)
        return {'x_q': jax.random.normal(k1, (B, Tq, EMBED_DIM), jnp.float32), 'x_kv': jax.random.normal(k2, (B, Tk, EMBED_DIM), jnp.float32), 'w_q': jax.random.normal(k3, (EMBED_DIM, EMBED_DIM), jnp.float32) * std, 'w_kv': jax.random.normal(k4, (EMBED_DIM, 2 * EMBED_DIM), jnp.float32) * std, 'w_proj': jax.random.normal(k5, (EMBED_DIM, EMBED_DIM), jnp.float32) * std, 'w_rel': jax.random.normal(k6, (1, NUM_HEADS), jnp.float32) * 0.02}
    _L0_xattn_all = _L0_xattn_setup()
    _L0_xattn_in = {k: v for k, v in _L0_xattn_all.items() if k in ('w_q', 'w_kv', 'w_proj', 'w_rel')}
    del _L0_xattn_all

    def _L0_ffn_setup():
        import jax, jax.numpy as jnp
        import numpy as np
        B, S, D, H, E = (4, 256, 128, 256, 8)
        key = jax.random.key(seed)
        ks = jax.random.split(key, 8)
        scale = 0.02
        return {'x': jax.random.normal(ks[0], (B, S, D), dtype=jnp.float32), 'Wr': jax.random.normal(ks[1], (D, E), dtype=jnp.float32) * scale, 'br': jnp.zeros((E,), dtype=jnp.float32), 'W1': jax.random.normal(ks[2], (E, D, H), dtype=jnp.float32) * scale, 'b1': jnp.zeros((E, H), dtype=jnp.float32), 'W2': jax.random.normal(ks[3], (E, H, D), dtype=jnp.float32) * scale, 'b2': jnp.zeros((E, D), dtype=jnp.float32)}
    _L0_ffn_all = _L0_ffn_setup()
    _L0_ffn_in = {k: v for k, v in _L0_ffn_all.items() if k in ('Wr', 'br', 'W1', 'b1', 'W2', 'b2')}
    del _L0_ffn_all

    def _L1_attn_setup():
        import jax, jax.numpy as jnp
        import numpy as np
        B, S, D_IN, D_OUT, H = (2, 256, 128, 128, 16)
        HD = D_OUT // H
        key = jax.random.key(seed)
        ks = jax.random.split(key, 6)
        s = 0.02
        return {'X': jax.random.normal(ks[0], (B, S, D_IN), dtype=jnp.float32), 'Wq': jax.random.normal(ks[1], (D_OUT, D_IN), dtype=jnp.float32) * s, 'Wk': jax.random.normal(ks[2], (D_OUT, D_IN), dtype=jnp.float32) * s, 'Wv': jax.random.normal(ks[3], (D_OUT, D_IN), dtype=jnp.float32) * s, 'Wo': jax.random.normal(ks[4], (D_OUT, D_OUT), dtype=jnp.float32) * s, 'bo': jax.random.normal(ks[5], (D_OUT,), dtype=jnp.float32) * s}
    _L1_attn_all = _L1_attn_setup()
    _L1_attn_in = {k: v for k, v in _L1_attn_all.items() if k in ('Wq', 'Wk', 'Wv', 'Wo', 'bo')}
    del _L1_attn_all

    def _L1_xattn_setup():
        import jax, jax.numpy as jnp
        import numpy as np
        EPS = 1e-05
        NEG = -1e+20

        def layer_norm(x, gamma, beta):
            mu = jnp.mean(x, axis=-1, keepdims=True)
            var = jnp.mean(jnp.square(x - mu), axis=-1, keepdims=True)
            return (x - mu) * jax.lax.rsqrt(var + EPS) * gamma + beta
        key = jax.random.key(seed)
        ks = jax.random.split(key, 12)
        B, S, D, H, HD = (2, 256, 128, 16, 64)
        hid = H * HD
        inp = {'q': jax.random.normal(ks[0], (B, S, D), jnp.float32), 'k': jax.random.normal(ks[1], (B, S, D), jnp.float32), 'v': jax.random.normal(ks[2], (B, S, D), jnp.float32), 'mask': jax.random.randint(ks[3], (B, 1, S, S), 0, 2, jnp.int32), 'Wq': jax.random.normal(ks[4], (D, hid), jnp.float32) * D ** (-0.5), 'bq': jnp.zeros((hid,), jnp.float32), 'Wk': jax.random.normal(ks[5], (D, hid), jnp.float32) * D ** (-0.5), 'bk': jnp.zeros((hid,), jnp.float32), 'Wv': jax.random.normal(ks[6], (D, hid), jnp.float32) * D ** (-0.5), 'bv': jnp.zeros((hid,), jnp.float32), 'Wo': jax.random.normal(ks[7], (hid, D), jnp.float32) * hid ** (-0.5), 'bo': jnp.zeros((D,), jnp.float32), 'gamma': jnp.ones((D,), jnp.float32), 'beta': jnp.zeros((D,), jnp.float32)}
        return inp
    _L1_xattn_all = _L1_xattn_setup()
    _L1_xattn_in = {k: v for k, v in _L1_xattn_all.items() if k in ('Wq', 'bq', 'Wk', 'bk', 'Wv', 'bv', 'Wo', 'bo', 'gamma', 'beta')}
    del _L1_xattn_all

    def _L1_ffn_setup():
        import jax, jax.numpy as jnp
        import numpy as np
        TOP_K = 32
        TEMPERATURE = 1.0
        PARAM_SCALE = 0.02

        def _compose_weight(logits, A, B):
            vals, idx = jax.lax.top_k(logits, TOP_K)
            w = jax.nn.softmax(vals / TEMPERATURE)
            A_sel = A[idx]
            B_sel = B[idx]
            return jnp.einsum('k,kir,kro->io', w, A_sel, B_sel)
        key = jax.random.key(seed)
        ks = jax.random.split(key, 7)
        B, S, D, F, P, R = (2, 128, 128, 512, 32, 64)
        x = jax.random.normal(ks[0], (B, S, D), dtype=jnp.float32)
        fc1_A = jax.random.normal(ks[1], (P, D, R), dtype=jnp.float32) * PARAM_SCALE
        fc1_B = jax.random.normal(ks[2], (P, R, F), dtype=jnp.float32) * PARAM_SCALE
        fc2_A = jax.random.normal(ks[3], (P, F, R), dtype=jnp.float32) * PARAM_SCALE
        fc2_B = jax.random.normal(ks[4], (P, R, D), dtype=jnp.float32) * PARAM_SCALE
        fc1_logits = jax.random.normal(ks[5], (P,), dtype=jnp.float32)
        fc2_logits = jax.random.normal(ks[6], (P,), dtype=jnp.float32)
        return {'x': x, 'fc1_A': fc1_A, 'fc1_B': fc1_B, 'fc2_A': fc2_A, 'fc2_B': fc2_B, 'fc1_logits': fc1_logits, 'fc2_logits': fc2_logits}
    _L1_ffn_all = _L1_ffn_setup()
    _L1_ffn_in = {k: v for k, v in _L1_ffn_all.items() if k in ('fc1_A', 'fc1_B', 'fc2_A', 'fc2_B', 'fc1_logits', 'fc2_logits')}
    del _L1_ffn_all
    return {'x': x, 'ctx_1024': ctx_1024, 'mask_Bx1xSxS2_ik1': mask_Bx1xSxS2_ik1, 'L0_attn_w_qkv': _L0_attn_in['w_qkv'], 'L0_attn_w_proj': _L0_attn_in['w_proj'], 'L0_xattn_w_q': _L0_xattn_in['w_q'], 'L0_xattn_w_kv': _L0_xattn_in['w_kv'], 'L0_xattn_w_proj': _L0_xattn_in['w_proj'], 'L0_xattn_w_rel': _L0_xattn_in['w_rel'], 'L0_ffn_Wr': _L0_ffn_in['Wr'], 'L0_ffn_br': _L0_ffn_in['br'], 'L0_ffn_W1': _L0_ffn_in['W1'], 'L0_ffn_b1': _L0_ffn_in['b1'], 'L0_ffn_W2': _L0_ffn_in['W2'], 'L0_ffn_b2': _L0_ffn_in['b2'], 'L1_attn_Wq': _L1_attn_in['Wq'], 'L1_attn_Wk': _L1_attn_in['Wk'], 'L1_attn_Wv': _L1_attn_in['Wv'], 'L1_attn_Wo': _L1_attn_in['Wo'], 'L1_attn_bo': _L1_attn_in['bo'], 'L1_xattn_Wq': _L1_xattn_in['Wq'], 'L1_xattn_bq': _L1_xattn_in['bq'], 'L1_xattn_Wk': _L1_xattn_in['Wk'], 'L1_xattn_bk': _L1_xattn_in['bk'], 'L1_xattn_Wv': _L1_xattn_in['Wv'], 'L1_xattn_bv': _L1_xattn_in['bv'], 'L1_xattn_Wo': _L1_xattn_in['Wo'], 'L1_xattn_bo': _L1_xattn_in['bo'], 'L1_xattn_gamma': _L1_xattn_in['gamma'], 'L1_xattn_beta': _L1_xattn_in['beta'], 'L1_ffn_fc1_A': _L1_ffn_in['fc1_A'], 'L1_ffn_fc1_B': _L1_ffn_in['fc1_B'], 'L1_ffn_fc2_A': _L1_ffn_in['fc2_A'], 'L1_ffn_fc2_B': _L1_ffn_in['fc2_B'], 'L1_ffn_fc1_logits': _L1_ffn_in['fc1_logits'], 'L1_ffn_fc2_logits': _L1_ffn_in['fc2_logits']}

def reference(x, ctx_1024, mask_Bx1xSxS2_ik1, L0_attn_w_qkv, L0_attn_w_proj, L0_xattn_w_q, L0_xattn_w_kv, L0_xattn_w_proj, L0_xattn_w_rel, L0_ffn_Wr, L0_ffn_br, L0_ffn_W1, L0_ffn_b1, L0_ffn_W2, L0_ffn_b2, L1_attn_Wq, L1_attn_Wk, L1_attn_Wv, L1_attn_Wo, L1_attn_bo, L1_xattn_Wq, L1_xattn_bq, L1_xattn_Wk, L1_xattn_bk, L1_xattn_Wv, L1_xattn_bv, L1_xattn_Wo, L1_xattn_bo, L1_xattn_gamma, L1_xattn_beta, L1_ffn_fc1_A, L1_ffn_fc1_B, L1_ffn_fc2_A, L1_ffn_fc2_B, L1_ffn_fc1_logits, L1_ffn_fc2_logits):
    import jax
    import jax.numpy as jnp

    def _L0_attn_ref(x, w_qkv, w_proj):
        import jax, jax.numpy as jnp
        import numpy as np
        B, N, DIM = (4, 512, 128)
        H, M = (16, 64)
        HD = DIM // H

        def iterative_inv(mat, n_iter=6):
            m = mat.shape[-1]
            I = jnp.eye(m, dtype=mat.dtype)
            K = mat
            denom = jnp.max(jnp.sum(K, axis=-2), axis=-1)[:, :, None, None]
            V = jnp.swapaxes(K, -1, -2) / denom
            for _ in range(n_iter):
                KV = jnp.matmul(K, V)
                V = jnp.matmul(0.25 * V, 13 * I - jnp.matmul(KV, 15 * I - jnp.matmul(KV, 7 * I - KV)))
            return V

        def _reference_tuple_inner(x, w_qkv, w_proj):
            b, n, c = x.shape
            qkv = (x @ w_qkv).reshape(b, n, 3, H, HD)
            qkv = jnp.transpose(qkv, (2, 0, 3, 1, 4))
            Q, K, V = (qkv[0], qkv[1], qkv[2])
            Q = Q / jnp.asarray(HD ** 0.5, dtype=Q.dtype)
            Q_l = Q.reshape(b, H, M, n // M, HD).mean(axis=-2)
            K_l = K.reshape(b, H, M, n // M, HD).mean(axis=-2)
            kernel1 = jax.nn.softmax(jnp.einsum('bhnd,bhmd->bhnm', Q, K_l), axis=-1)
            kernel2 = jax.nn.softmax(jnp.einsum('bhmd,bhkd->bhmk', Q_l, K_l), axis=-1)
            kernel3 = jax.nn.softmax(jnp.einsum('bhmd,bhnd->bhmn', Q_l, K), axis=-1)
            SV = jnp.matmul(jnp.matmul(kernel1, iterative_inv(kernel2)), jnp.matmul(kernel3, V))
            SV = jnp.transpose(SV, (0, 2, 1, 3)).reshape(b, n, c)
            out = SV @ w_proj
            return (out, SV)
        return _reference_tuple_inner(x, w_qkv, w_proj)[0]

    def _L0_xattn_ref(x_q, x_kv, w_q, w_kv, w_proj, w_rel):
        import jax, jax.numpy as jnp
        import numpy as np
        EMBED_DIM = 128
        NUM_HEADS = 16
        HEAD_DIM = EMBED_DIM // NUM_HEADS
        SCALE = HEAD_DIM ** (-0.5)
        B, Tq, _ = x_q.shape
        Tk = x_kv.shape[1]
        q = x_q @ w_q
        kv = x_kv @ w_kv
        k, v = jnp.split(kv, 2, axis=-1)

        def heads(y, T):
            return y.reshape(B, T, NUM_HEADS, HEAD_DIM).transpose(0, 2, 1, 3)
        q = heads(q, Tq)
        k = heads(k, Tk)
        v = heads(v, Tk)
        logits = jnp.einsum('bhqd,bhkd->bhqk', q, k) * SCALE
        rel = jnp.arange(Tq, dtype=jnp.float32)[:, None] - jnp.arange(Tk, dtype=jnp.float32)[None, :]
        bias = rel[..., None] * w_rel[0]
        bias = bias.transpose(2, 0, 1)[None]
        logits = logits + bias
        attn = jax.nn.softmax(logits, axis=-1)
        out = jnp.einsum('bhqk,bhkd->bhqd', attn, v)
        out = out.transpose(0, 2, 1, 3).reshape(B, Tq, EMBED_DIM)
        return out @ w_proj

    def _L0_ffn_ref(x, Wr, br, W1, b1, W2, b2):
        import jax, jax.numpy as jnp
        import numpy as np
        B, S, D, H, E = (4, 256, 128, 256, 8)
        d = x.shape[-1]
        tokens = x.reshape(-1, d)
        logits = tokens @ Wr + br
        probs = jax.nn.softmax(logits, axis=-1)
        expert = jnp.argmax(probs, axis=-1)
        max_prob = jnp.take_along_axis(probs, expert[:, None], axis=-1)
        h = jax.nn.relu(jnp.einsum('td,edh->teh', tokens, W1) + b1[None])
        y = jnp.einsum('teh,ehd->ted', h, W2) + b2[None]
        out = jnp.take_along_axis(y, expert[:, None, None], axis=1)[:, 0, :]
        return (out * max_prob).reshape(x.shape)

    def _L1_attn_ref(X, Wq, Wk, Wv, Wo, bo):
        import jax, jax.numpy as jnp
        import numpy as np
        B, S, D_IN, D_OUT, H = (2, 256, 128, 128, 16)
        HD = D_OUT // H
        b, n, _ = X.shape
        Q = (X @ Wq.T).reshape(b, n, H, HD).transpose(0, 2, 1, 3)
        K = (X @ Wk.T).reshape(b, n, H, HD).transpose(0, 2, 1, 3)
        V = (X @ Wv.T).reshape(b, n, H, HD).transpose(0, 2, 1, 3)
        S_ = jnp.einsum('bhqd,bhkd->bhqk', Q, K)
        causal = jnp.triu(jnp.ones((n, n), dtype=bool), k=1)
        S_ = jnp.where(causal, -jnp.inf, S_)
        W = jax.nn.softmax(S_ / jnp.sqrt(jnp.float32(HD)), axis=-1)
        Z = jnp.einsum('bhqk,bhkd->bhqd', W, V)
        Z = Z.transpose(0, 2, 1, 3).reshape(b, n, D_OUT)
        return Z @ Wo.T + bo

    def _L1_xattn_ref(q, k, v, mask, Wq, bq, Wk, bk, Wv, bv, Wo, bo, gamma, beta):
        import jax, jax.numpy as jnp
        import numpy as np
        EPS = 1e-05
        NEG = -1e+20

        def layer_norm(x, gamma, beta):
            mu = jnp.mean(x, axis=-1, keepdims=True)
            var = jnp.mean(jnp.square(x - mu), axis=-1, keepdims=True)
            return (x - mu) * jax.lax.rsqrt(var + EPS) * gamma + beta
        B, S, D = q.shape
        H, HD = (16, 64)
        scale = HD ** (-0.5)
        qh = (layer_norm(q, gamma, beta) @ Wq + bq).reshape(B, S, H, HD).transpose(0, 2, 1, 3)
        kh = (layer_norm(k, gamma, beta) @ Wk + bk).reshape(B, S, H, HD).transpose(0, 2, 1, 3)
        vh = (layer_norm(v, gamma, beta) @ Wv + bv).reshape(B, S, H, HD).transpose(0, 2, 1, 3)
        dots = jnp.einsum('bhqd,bhkd->bhqk', qh, kh)
        dots = jnp.where(mask == 0, NEG, dots) * scale
        attn = jax.nn.softmax(dots, axis=-1)
        out = jnp.einsum('bhqk,bhkd->bhqd', attn, vh)
        out = out.reshape(B, S, H * HD)
        return out @ Wo + bo

    def _L1_ffn_ref(x, fc1_A, fc1_B, fc2_A, fc2_B, fc1_logits, fc2_logits):
        import jax, jax.numpy as jnp
        import numpy as np
        TOP_K = 32
        TEMPERATURE = 1.0
        PARAM_SCALE = 0.02

        def _compose_weight(logits, A, B):
            vals, idx = jax.lax.top_k(logits, TOP_K)
            w = jax.nn.softmax(vals / TEMPERATURE)
            A_sel = A[idx]
            B_sel = B[idx]
            return jnp.einsum('k,kir,kro->io', w, A_sel, B_sel)
        W1 = _compose_weight(fc1_logits, fc1_A, fc1_B)
        W2 = _compose_weight(fc2_logits, fc2_A, fc2_B)
        h = jax.nn.gelu(jnp.einsum('bsd,df->bsf', x, W1))
        return jnp.einsum('bsf,fd->bsd', h, W2)
    x = _layernorm(x + _L0_attn_ref(x, L0_attn_w_qkv, L0_attn_w_proj), axis=-1)
    x = _layernorm(x + _L0_xattn_ref(x, ctx_1024, L0_xattn_w_q, L0_xattn_w_kv, L0_xattn_w_proj, L0_xattn_w_rel), axis=-1)
    x = _layernorm(x + _L0_ffn_ref(x, L0_ffn_Wr, L0_ffn_br, L0_ffn_W1, L0_ffn_b1, L0_ffn_W2, L0_ffn_b2), axis=-1)
    x = _layernorm(x + _L1_attn_ref(x, L1_attn_Wq, L1_attn_Wk, L1_attn_Wv, L1_attn_Wo, L1_attn_bo), axis=-1)
    x = _layernorm(x + _L1_xattn_ref(x, ctx_1024, ctx_1024, mask_Bx1xSxS2_ik1, L1_xattn_Wq, L1_xattn_bq, L1_xattn_Wk, L1_xattn_bk, L1_xattn_Wv, L1_xattn_bv, L1_xattn_Wo, L1_xattn_bo, L1_xattn_gamma, L1_xattn_beta), axis=-1)
    x = _layernorm(x + _L1_ffn_ref(x, L1_ffn_fc1_A, L1_ffn_fc1_B, L1_ffn_fc2_A, L1_ffn_fc2_B, L1_ffn_fc1_logits, L1_ffn_fc2_logits), axis=-1)
    return x

_drawn_inputs = setup_inputs


def setup_inputs(seed=0):
    import zlib

    import numpy as np

    out = dict(_drawn_inputs(seed))
    spreads = {'L0_ffn_br': (0.0, 0.472),
     'L0_ffn_b1': (0.0, 0.8),
     'L0_ffn_b2': (0.0, 0.523),
     'L1_xattn_bq': (0.0, 0.475),
     'L1_xattn_bk': (0.0, 0.8),
     'L1_xattn_bv': (0.0, 0.1),
     'L1_xattn_bo': (0.0, 0.1),
     'L1_xattn_gamma': (1.0, 0.2),
     'L1_xattn_beta': (0.0, 0.1)}
    factors = {'L0_attn_w_qkv': 8.0,
     'L0_attn_w_proj': 8.0,
     'L0_ffn_Wr': 3.519,
     'L0_ffn_W1': 8.0,
     'L0_ffn_W2': 6.331,
     'L1_attn_Wq': 8.0,
     'L1_attn_Wk': 8.0,
     'L1_attn_Wv': 2.667,
     'L1_attn_bo': 2.748,
     'L1_ffn_fc1_A': 8.0,
     'L1_ffn_fc1_B': 8.0,
     'L1_ffn_fc2_A': 8.0,
     'L1_ffn_fc2_B': 8.0,
     'L1_ffn_fc1_logits': 8.0,
     'L1_ffn_fc2_logits': 8.0}
    for name, (base, spread) in spreads.items():
        noise = np.random.default_rng([zlib.crc32(name.encode()), seed]).standard_normal(out[name].shape)
        drawn = base * np.exp(spread * noise) if base else spread * noise
        out[name] = jnp.asarray(drawn.astype(out[name].dtype))
    for name, factor in factors.items():
        out[name] = (out[name] * factor).astype(out[name].dtype)
    return out
```

```python
from contextlib import ExitStack

import numpy as np

import concourse.bass as bass
from concourse import mybir

F32 = mybir.dt.float32
BF16 = mybir.dt.bfloat16
I32 = mybir.dt.int32
ALU = mybir.AluOpType
ACT = mybir.ActivationFunctionType
AX = mybir.AxisListType.X

B, S, D = 32, 128, 128
LANES = 2
H, HD = 16, 8
TG, TJ, TW = 4, 4, 32
M = 64
PAIRS = H // 2
NEWTON = 6
EXPERTS, HID = 8, 256
XH, XHD = 16, 64
PRIM, RANK, FF = 32, 64, 512
EPS = 1e-5
SC8 = float(HD) ** -0.5
SC64 = float(XHD) ** -0.5
NEG = -1e20
GELU_C, GELU_A = 0.7978845608028654, 0.044715

WEIGHTS = [
    ("n_q4", 512), ("n_k4", 512), ("n_v", D), ("n_p", D),
    ("x_q4", 512), ("x_k4", 512), ("x_v", D), ("x_p", D),
    ("c_q4", 512), ("c_k4", 512), ("c_v", D), ("c_p", D),
    ("m_r", EXPERTS), ("m_1", EXPERTS * HID), ("m_2", EXPERTS * HID),
    ("y_q", XH * XHD), ("y_k", XH * XHD), ("y_v", XH * XHD), ("y_p", XH * XHD),
    ("m_b1", 16), ("y_bq", 8), ("y_bk", 8), ("y_g", 1), ("y_b", 1), ("x_rel", TG),
    ("ident", 128), ("ones2", 128), ("ident2", M), ("qaug", 128), ("kpat", 128), ("kpos", 128),
    ("causal", 128), ("first", EXPERTS), ("mhalf", 1),
]
WCOL = {}
for _n, _w in WEIGHTS:
    WCOL[_n] = (sum(w for _, w in WEIGHTS[:len(WCOL)]), _w)
NW = sum(w for _, w in WEIGHTS)
ROWS = [("m_br", EXPERTS), ("c_bo", D), ("y_bo", D), ("y_bv", XH * XHD), ("l1", PRIM), ("l2", PRIM)]
RCOL = {}
for _n, _w in ROWS:
    RCOL[_n] = (sum(w for _, w in ROWS[:len(RCOL)]), _w)
NR = sum(w for _, w in ROWS)


def build(nc, x, xT, ctx, ctxT, mask, wpack, rows, b2, a1, b1, a2, b2w, out):
    with ExitStack() as top:
        def sb(name, shape, dt=F32, scope=top):
            return scope.enter_context(nc.sbuf_tensor(name, shape, dt))

        W = sb("weights", [128, NW])
        R = sb("row_weights", [128, NR])
        b2s = sb("expert_b2", [EXPERTS, D])
        F1 = sb("ffn_w1", [128, FF])
        F2 = sb("ffn_w2", [128, 4, D])
        kaug = sb("kaug", [128, TG, 128])
        ident_bf = sb("ident_bf", [128, 128], BF16)
        causal_bf = sb("causal_bf", [128, 128], BF16)

        def w(name, a=0, n=None):
            c, width = WCOL[name]
            return W[:, c + a:c + a + (width - a if n is None else n)]

        def row(name):
            c, width = RCOL[name]
            return R[:, c:c + width]

        ident = w("ident")
        lanes = range(LANES)
        def lane(name, shape, dt=F32):
            return [sb(f"{name}{s}", shape, dt) for s in lanes]

        v9 = lane("v9", [128, H, TW])
        w9 = lane("w9", [128, PAIRS, TW])
        PS = [top.enter_context(nc.psum_tensor(f"ps{s}", [128, 4, 512], F32)) for s in lanes]

        def sm(s, name, a=0, n=None):
            place = {"mx1": (0, 16), "mx2": (16, 8), "mx3": (24, 8), "rs2": (32, 8), "rd": (40, 8),
                     "rs3": (48, 8), "mx": (56, 16), "nb": (72, 16), "rs": (88, 16), "st": (104, 6),
                     "mv": (110, 2), "ve": (112, 1), "rstd": (113, 1), "cst": (114, 6), "cmv": (120, 2),
                     "cve": (122, 1), "crstd": (123, 1), "lg": (124, 8), "e8": (132, 8), "gate": (140, 8),
                     "pmx": (148, 1), "pnb": (149, 1), "psum": (150, 1), "emx": (151, 1), "fmx": (152, 1),
                     "grs": (153, 1), "gp": (154, 1)}
            c, width = place[name]
            return small[s][:, c + a:c + a + (width - a if n is None else n)]

        def over(ap, n):
            return ap.unsqueeze(2).to_broadcast([128, ap.shape[1], n])

        def every(ap, n):
            return ap.unsqueeze(1).to_broadcast([128, n, ap.shape[1]])

        with ExitStack() as pre:
            A1 = sb("fc1_A", [128, 16, D], scope=pre)
            B1 = sb("fc1_B", [128, 16, FF], scope=pre)
            A2 = sb("fc2_A", [128, 16, FF], scope=pre)
            B2 = sb("fc2_B", [128, 16, D], scope=pre)
            lw = sb("mix", [128, 2, PRIM], scope=pre)
            lcol = sb("mix_col", [128, 2, 16], scope=pre)
            tmp = sb("mix_tmp", [128, 8], scope=pre)

            pre_sems = []

            def sem(name):
                pre_sems.append(nc.alloc_semaphore(name))
                return pre_sems[-1]
            weights_in, rows_in, fc_in = sem("weights_in"), sem("rows_in"), sem("fc_in")
            steps, mixed, scaled, composed = sem("pre_steps"), sem("mixed"), sem("scaled"), sem("composed")
            mix_max, cleared = sem("mix_max"), sem("cleared")
            block = nc.Block()
            pre.enter_context(block)

            @block.sync
            def _(sp):
                sp.dma_start(R[:], rows.to_broadcast([128, NR])).then_inc(rows_in, 16)
                sp.dma_start(W[:], wpack).then_inc(weights_in, 16)
                sp.dma_start(b2s[:], b2).then_inc(weights_in, 16)
                for n, (dst, src) in enumerate(((A1, a1), (B1, b1), (A2, a2), (B2, b2w))):
                    sp.dma_start(dst[:], src).then_inc(fc_in, 16)
                sp.wait_ge(fc_in, 64)
                sp.wait_ge(weights_in, 32)

            @block.scalar
            def _(act):
                act.wait_ge(mix_max, 1)
                for n in range(2):
                    nc.scalar.activation(lw[:, n], row(f"l{n + 1}"), ACT.Exp, bias=tmp[:, 2 + n:3 + n],
                                         accum_out=tmp[:, 4 + n:5 + n]).then_inc(mixed, 1)

            @block.vector
            def _(dve):
                count = [0]

                def link(ins):
                    count[0] += 1
                    ins.then_inc(steps, 1)
                    dve.wait_ge(steps, count[0])

                for s in lanes:
                    nc.vector.memset(v9[s][:], 0.0)
                    link(nc.vector.memset(w9[s][:], 0.0))
                    nc.vector.memset(v9[s][:, :, HD:HD + 1], 1.0)
                    link(nc.vector.memset(w9[s][:, :, HD:HD + 1], 1.0))
                dve.wait_ge(rows_in, 16)
                for n in range(2):
                    nc.vector.tensor_reduce(tmp[:, n:n + 1], row(f"l{n + 1}"), AX, ALU.max).then_inc(cleared, 1)
                dve.wait_ge(cleared, 2)
                nc.vector.tensor_scalar(tmp[:, 2:4], tmp[:, 0:2], -1.0, None, ALU.mult).then_inc(mix_max, 1)
                dve.wait_ge(mixed, 2)
                link(nc.vector.reciprocal(tmp[:, 6:8], tmp[:, 4:6]))
                link(nc.vector.tensor_scalar(tmp[:, 7:8], tmp[:, 7:8], 0.5, None, ALU.mult))
                for n in range(2):
                    for half in range(2):
                        p = slice(64 * half, 64 * half + 64)
                        ins = nc.vector.tensor_scalar(lcol[p, n, :], lw[p, n, half:PRIM:2],
                                                      tmp[p, 6 + n:7 + n], None, ALU.mult)
                link(ins)
                dve.wait_ge(fc_in, 64)
                for n, a in ((0, A1), (1, B2)):
                    nc.vector.tensor_tensor(a[:], a[:], over(lcol[:, n], D), ALU.mult).then_inc(scaled, 1)
                dve.wait_ge(weights_in, 32)
                for g in range(TG):
                    link(nc.vector.tensor_tensor(kaug[:, g], w("kpat"), w("kpos"), ALU.mult))
                    link(nc.vector.tensor_scalar(kaug[:, g], kaug[:, g], w("x_rel", g, 1), 1.0 / SC8,
                                                 ALU.mult, ALU.mult))
                nc.vector.tensor_copy(ident_bf[:], ident)
                nc.vector.tensor_copy(causal_bf[:], w("causal"))
                dve.wait_ge(composed, 2)
                nc.vector.tensor_copy(F1[:], PS[0][:, 0])
                nc.vector.tensor_copy(F2[:], PS[0][:, 1].rearrange("p (f n) -> p f n", f=4))
                dve.drain()

            @block.tensor
            def _(pe):
                pe.wait_ge(scaled, 1)
                for c in range(16):
                    mm = nc.tensor.matmul(PS[0][:, 0], A1[:, c], B1[:, c], start=(c == 0), stop=(c == 15))
                mm.then_inc(composed, 1)
                pe.wait_ge(scaled, 2)
                for f in range(4):
                    for c in range(16):
                        mm = nc.tensor.matmul(PS[0][:, 1, 128 * f:128 * f + 128],
                                              A2[:, c, 128 * f:128 * f + 128], B2[:, c],
                                              start=(c == 0), stop=(c == 15))
                mm.then_inc(composed, 1)

        nc.clear_and_free_semaphores(pre_sems)
        nc.all_engine_barrier()

        xs = lane("x_rows", [128, D])
        xTs = lane("x_T", [128, 128])
        cs = lane("ctx_rows", [128, D])
        cTs = lane("ctx_T", [128, 128])
        ms = lane("mask_i", [128, 128], I32)
        madd = lane("mask_add", [128, 128], BF16)
        q4 = lane("q4", [128, TG, 128])
        kk = lane("kk", [128, TG, M + 128])
        ql = lane("q_landmarks", [128, TG, M])
        e1 = lane("e1", [128, H, M])
        p2 = lane("p2", [128, PAIRS, M])
        e3 = lane("e3", [128, PAIRS, 128])
        e1T = lane("e1T", [128, PAIRS, 128])
        e3T = lane("e3T", [128, PAIRS, 128])
        k2T = lane("k2T", [128, 4, 128])
        ey = [[sb(f"ey{s}{g}", [128, 4, M + HD]) for g in range(2)] for s in lanes]
        ss = [[sb(f"ss{s}{g}", [128, 4, M + HD]) for g in range(2)] for s in lanes]
        wz = [[sb(f"wz{s}{g}", [128, 4, M + HD]) for g in range(2)] for s in lanes]
        uu = [[sb(f"uu{s}{g}", [128, 4, HD]) for g in range(2)] for s in lanes]
        pe_ = [[sb(f"probs{s}{g}", [128, 4, 128]) for g in range(2)] for s in lanes]
        pT = [[sb(f"probsT{s}{g}", [128, 4, 128]) for g in range(2)] for s in lanes]
        small = lane("small", [128, 160])
        oT = lane("oT", [128, TG, 128])
        z = lane("z", [128, H, HD])
        zT = lane("zT", [128, 128])
        res = lane("res", [128, D])
        xbo = lane("x_plus_bo", [128, D])
        cn = lane("ctx_norm", [128, D])
        xn = lane("x_norm", [128, D])
        cnT = lane("ctx_normT", [128, 128])
        xnT = lane("x_normT", [128, 128])
        q8, k8, o8 = e1T, e3, e3T
        v8 = lane("v8", [128, 2, 512])
        hT = [[sb(f"hT{s}{g}", [128, 4, 128]) for g in range(2)] for s in lanes]
        gT = lane("gateT", [EXPERTS, 128])

        def end(names):
            nc.clear_and_free_semaphores([made.pop(key) for key in names])
            nc.all_engine_barrier()

        def sem(name, s=0):
            key = f"{name}{s}"
            if key not in made:
                made[key] = nc.alloc_semaphore(key)
            return made[key]

        made = {}
        with nc.Fori(0, B // LANES) as turn:
            with nc.Block() as block:
                body(nc, block, "nystrom", turn, sem, lanes, dict(locals()))
            end([key for key in made if key.startswith("n_")])
            with nc.Block() as block:
                body(nc, block, "rest", turn, sem, lanes, dict(locals()))
            end(list(made))


def body(nc, block, part, turn, sem, lanes, o):
    (x, xT, ctx, ctxT, mask, out, W, R, b2s, F1, F2, kaug, ident_bf, causal_bf, w, row, ident) = (
        o[k] for k in "x xT ctx ctxT mask out W R b2s F1 F2 kaug ident_bf causal_bf w row ident".split())
    (xs, xTs, cs, cTs, ms, madd, q4, kk, ql, v9, w9, e1, p2, e3, e1T, e3T, k2T, ey, ss, wz, uu, pe_, pT) = (
        o[k] for k in "xs xTs cs cTs ms madd q4 kk ql v9 w9 e1 p2 e3 e1T e3T k2T ey ss wz uu pe_ pT".split())
    (oT, z, zT, res, xbo, cn, xn, cnT, xnT, q8, k8, v8, o8, hT, gT, PS, sm, over, every) = (
        o[k] for k in "oT z zT res xbo cn xn cnT xnT q8 k8 v8 o8 hT gT PS sm over every".split())

    def bank(s, b, a=0, n=512):
        return PS[s][:, b, a:a + n]

    def heads(h):
        g, j = divmod(h, TJ)
        p, m = divmod(h, 2)
        return g, slice(TW * j, TW * j + TW), p, slice(M * m, M * m + M)

    members = [(i, slice(M * m, M * m + M)) for i in range(4) for m in range(2)]

    @block.sync
    def _(sp):
        if part == "nystrom":
          for s in lanes:
            sp.dma_start(xTs[s][:], xT[turn * LANES + s]).then_inc(sem("xT_in", s), 16)
            sp.dma_start(xs[s][:], x[turn * LANES + s]).then_inc(sem("x_in", s), 16)
          for s in lanes:
            sp.dma_start(cTs[s][:], ctxT[turn * LANES + s]).then_inc(sem("ctx_in", s), 16)
            sp.dma_start(cs[s][:], ctx[turn * LANES + s]).then_inc(sem("ctx_in", s), 16)
            sp.dma_start(ms[s][:], mask[turn * LANES + s]).then_inc(sem("ctx_in", s), 16)
          return
        for s in lanes:
            sp.wait_ge(sem("ln_rows", s), 6)
            sp.dma_start(out[turn * LANES + s], xs[s][:]).then_inc(sem("stored", s), 16)
        for s in lanes:
            sp.wait_ge(sem("stored", s), 16)

    @block.tensor
    def _(pe):
        mmul = nc.tensor.matmul

        def one(dst, lhsT, rhs):
            return mmul(dst, lhsT, rhs, start=True, stop=True)

        def turned(dst, src):
            return nc.tensor.transpose(dst, src, ident)

        def project(s, wq, wk, wv, src, sig):
            for b, (name, t) in enumerate(((wq, xTs[s]), (wk, src))):
                for g in range(TG):
                    mm = one(bank(s, b, 128 * g, 128), w(name, 128 * g, 128), t[:])
                mm.then_inc(sem(sig, s), 1)
            one(bank(s, 2, 0, D), src[:], w(wv)).then_inc(sem(sig, s), 1)

        def tail_turn(s, n):
            pe.wait_ge(sem("oT", s), n)
            for g in range(TG):
                mm = turned(bank(s, 0, 128 * g, 128), oT[s][:, g])
            mm.then_inc(sem("o_rows", s), 1)

        def tail_zT(s, n):
            pe.wait_ge(sem("z", s), n)
            turned(bank(s, 2, 0, 128), z[s][:].rearrange("p h e -> p (h e)")).then_inc(sem("zT_ps", s), 1)

        def tail_out(s, n, wp):
            pe.wait_ge(sem("zT", s), n)
            one(bank(s, 2, 128, D), zT[s][:], w(wp)).then_inc(sem("sub", s), 1)

        def ln_turn(s, n):
            pe.wait_ge(sem("ln_rows", s), n)
            turned(bank(s, 0, 0, 128), xs[s][:]).then_inc(sem("ln_T_ps", s), 1)

        if part == "nystrom":
            for s in lanes:
                pe.wait_ge(sem("xT_in", s), 16)
                project(s, "n_q4", "n_k4", "n_v", xTs[s], "n_proj")
            for s in lanes:
                pe.wait_ge(sem("n_lm", s), 2)
                for j in range(2):
                    n_k1(nc, sem, s, j, PS, q4, kk)
                pe.wait_ge(sem("n_v9", s), 1)
                for t in range(2):
                    n_k23(nc, sem, s, t, PS, ql, kk)
            for j in range(2, TJ):
                for s in lanes:
                    pe.wait_ge(sem("n_s1", s), j - 1)
                    n_k1(nc, sem, s, j, PS, q4, kk)
            for t in range(2, 4):
                for s in lanes:
                    pe.wait_ge(sem("n_s23", s), t - 1)
                    n_k23(nc, sem, s, t, PS, ql, kk)
            for s in lanes:
                pe.wait_ge(sem("n_s1", s), 4)
                for half in range(2):
                    pe.wait_ge(sem("n_p2", s), half + 1)
                    one(bank(s, 0, 256 * half, 256), w("ones2"),
                        p2[s][:, 4 * half:4 * half + 4].rearrange("p a b -> p (a b)")).then_inc(sem("n_colsum", s), 1)
                    for i in (2 * half, 2 * half + 1):
                        mm = turned(bank(s, 1, 128 * i, 128), p2[s][:, 2 * i:2 * i + 2].rearrange("p a b -> p (a b)"))
                    mm.then_inc(sem("n_k2T_ps", s), 1)
            for s in lanes:
                pe.wait_ge(sem("n_s23", s), 4)
                pe.wait_ge(sem("n_e23", s), 2)
                for p in range(PAIRS):
                    mm = turned(bank(s, 2 + p // 4, 128 * (p % 4), 128), e3[s][:, p])
                    if p % 4 == 3:
                        mm.then_inc(sem("n_e3T_ps", s), 1)
            for s in lanes:
                pe.wait_ge(sem("n_e1", s), 4)
                for p in range(PAIRS):
                    if p % 4 == 0:
                        pe.wait_ge(sem("n_e3T", s), p // 4 + 1)
                    mm = turned(bank(s, 2 + p // 4, 128 * (p % 4), 128),
                                e1[s][:, 2 * p:2 * p + 2].rearrange("p a b -> p (a b)"))
                    if p % 4 == 3:
                        mm.then_inc(sem("n_e1T_ps", s), 1)
            for s in lanes:
                pe.wait_ge(sem("n_rd", s), 1)
                pe.wait_ge(sem("n_k2T", s), 1)
                for g in range(2):
                    for i, m in members:
                        t = k2T[s][M * g:M * g + M, i, m]
                        mm = one(PS[s][m, g, 72 * i:72 * i + M], t, t)
                    mm.then_inc(sem("n_kkT", s), 1)
                pe.wait_ge(sem("n_e1T", s), 2)
                for h in range(H):
                    _, _, p, m = heads(h)
                    mm = one(PS[s][m, 2, 16 * p:16 * p + HD + 1], e3T[s][:, p, m], v9[s][:, h, 0:HD + 1])
                mm.then_inc(sem("n_y0", s), 1)
            for k in range(NEWTON):
                for g in range(2):
                    for s in lanes:
                        pe.wait_ge(sem("n_e", s), 2 * k + g + 1)
                        pe.wait_ge(sem("n_y", s), 2 * k + g + 1)
                        for i, m in members:
                            mm = one(PS[s][m, g, 72 * i:72 * i + 72], ey[s][g][m, i, 0:M], ey[s][g][m, i])
                        mm.then_inc(sem("n_S_ps", s), 1)
                for g in range(2):
                    for s in lanes:
                        pe.wait_ge(sem("n_S", s), 2 * k + g + 1)
                        pe.wait_ge(sem("n_wz", s), 2 * k + g + 1)
                        a = 0 if k < NEWTON - 1 else M
                        for i, m in members:
                            mm = one(PS[s][m, 2 + g, 72 * i + a:72 * i + 72], ss[s][g][m, i, 0:M], wz[s][g][m, i, a:72])
                        mm.then_inc(sem("n_SW", s), 1)
            for s in lanes:
                pe.wait_ge(sem("n_y", s), 2 * NEWTON + 2)
                for h in range(H):
                    _, _, p, m = heads(h)
                    mm = one(PS[s][m, 0, 16 * p:16 * p + HD], p2[s][m, p], ey[s][p % 2][m, p // 2, M:M + HD])
                mm.then_inc(sem("n_w_ps", s), 1)
            for s in lanes:
                pe.wait_ge(sem("n_w9", s), 1)
                for h in range(H):
                    g, r, p, m = heads(h)
                    mm = one(PS[s][r, 3, 128 * g:128 * g + 128], w9[s][m, p], e1T[s][m, p])
                mm.then_inc(sem("o_ps", s), 1)
            for s in lanes:
                tail_turn(s, 1)
            for s in lanes:
                tail_zT(s, 1)
            for s in lanes:
                tail_out(s, 1, "n_p")
            for s in lanes:
                ln_turn(s, 1)

            return

        def attention8(names, srcs, n_ln, n_att, masked):
            for s in lanes:
                pe.wait_ge(sem("xT", s), n_ln)
                if srcs is cTs:
                    pe.wait_ge(sem("ctx_in", s), 48)
                project(s, *names[:3], srcs[s], "a_proj")

            def scores(s, g):
                if g == 0:
                    pe.wait_ge(sem("a_qk", s), 2 * n_att)
                if g >= 2:
                    pe.wait_ge(sem("a_p", s), 4 * (n_att - 1) + g - 1)
                if masked:
                    mmul(bank(s, g % 2).rearrange("p (a b) -> p a b", a=4), ident_bf[:],
                         every(causal_bf[:], 4), start=True, stop=False, skip_group_check=True)
                r = slice(TW * g, TW * g + TW)
                for i in range(TG):
                    mm = mmul(bank(s, g % 2, 128 * i, 128), q4[s][r, i], kk[s][r, i, M:M + 128],
                              start=not masked, stop=True, skip_group_check=True)
                mm.then_inc(sem("a_s", s), 1)

            def turn_probs(s, g):
                pe.wait_ge(sem("a_p", s), 4 * (n_att - 1) + g + 1)
                if g == 0:
                    pe.wait_ge(sem("a_v9", s), n_att)
                else:
                    pe.wait_ge(sem("a_pT", s), 4 * (n_att - 1) + g)
                for j in range(TJ):
                    mm = turned(bank(s, 2, 128 * j, 128), pe_[s][g % 2][:, j])
                mm.then_inc(sem("a_pT_ps", s), 1)

            def values(s, g):
                pe.wait_ge(sem("a_pT", s), 4 * (n_att - 1) + g + 1)
                for i in range(TG):
                    mm = one(PS[s][TW * i:TW * i + TW, 3, 128 * g:128 * g + 128], v9[s][:, TJ * i + g], pT[s][g % 2][:, i])
                mm.then_inc(sem("a_pv", s), 1)

            for s in lanes:
                scores(s, 0)
            for g in range(TG):
                for s in lanes:
                    if g + 1 < TG:
                        scores(s, g + 1)
                for s in lanes:
                    turn_probs(s, g)
                for s in lanes:
                    values(s, g)
            for s in lanes:
                tail_turn(s, 1 + n_att)
            for s in lanes:
                tail_zT(s, 1 + n_att)
            for s in lanes:
                tail_out(s, 1 + n_att, names[3])

        attention8(("x_q4", "x_k4", "x_v", "x_p"), cTs, 1, 1, False)
        for s in lanes:
            ln_turn(s, 2)

        for s in lanes:
            pe.wait_ge(sem("xT", s), 2)
            one(bank(s, 3, 0, EXPERTS), xTs[s][:], w("m_r")).then_inc(sem("m_logits", s), 1)

        def hidden(s, t):
            if t >= 2:
                pe.wait_ge(sem(f"m_h{t % 2}", s), 1)
            for c in range(4):
                mm = one(bank(s, t % 2, 128 * c, 128), w("m_1", 512 * t + 128 * c, 128), xTs[s][:])
            mm.then_inc(sem("m_h_ps", s), 1)

        for s in lanes:
            hidden(s, 0)
        for t in range(4):
            for s in lanes:
                if t < 3:
                    hidden(s, t + 1)
            for s in lanes:
                pe.wait_ge(sem(f"m_h{t % 2}", s), t // 2 + 1)
                if t == 1:
                    pe.wait_ge(sem("m_res", s), 1)
                if t >= 2:
                    pe.wait_ge(sem("m_y_used", s), 2 * (t - 1))
                for e in (2 * t, 2 * t + 1):
                    for c in range(2):
                        mm = mmul(bank(s, 2 + t % 2, 128 * (e % 2), 128), hT[s][t % 2][:, 2 * (e % 2) + c],
                                  w("m_2", (2 * e + c) * 128, 128), start=(c == 0), stop=(c == 1))
                mm.then_inc(sem("m_y", s), 1)
            if t == 0:
                for s in lanes:
                    pe.wait_ge(sem("m_gate", s), 1)
                    turned(PS[s][0:EXPERTS, 3, 128:256], sm(s, "gate")).then_inc(sem("m_gT_ps", s), 1)
                for s in lanes:
                    pe.wait_ge(sem("m_gT", s), 1)
                    one(bank(s, 3, 256, D), gT[s][:], b2s[:]).then_inc(sem("m_b2", s), 1)
        for s in lanes:
            ln_turn(s, 3)

        attention8(("c_q4", "c_k4", "c_v", "c_p"), xTs, 3, 2, True)
        for s in lanes:
            ln_turn(s, 4)

        for s in lanes:
            pe.wait_ge(sem("y_cn", s), 1)
            turned(bank(s, 1, 0, 128), cn[s][:]).then_inc(sem("y_cnT_ps", s), 1)
            pe.wait_ge(sem("y_xn", s), 1)
            turned(bank(s, 1, 128, 128), xn[s][:]).then_inc(sem("y_xnT_ps", s), 1)
        for s in lanes:
            pe.wait_ge(sem("y_T", s), 2)
            pe.wait_ge(sem("xT", s), 4)
            for b, (name, t) in enumerate((("y_q", xnT[s]), ("y_q", xnT[s]), ("y_k", cnT[s]), ("y_k", cnT[s]))):
                for c in range(4):
                    mm = one(bank(s, b, 128 * c, 128), w(name, 512 * (b % 2) + 128 * c, 128), t[:])
                mm.then_inc(sem("y_qk_ps", s), 1)
        for s in lanes:
            for b in range(2):
                pe.wait_ge(sem("y_qk", s), b + 1)
                one(bank(s, b), cnT[s][:], w("y_v", 512 * b, 512)).then_inc(sem("y_v_ps", s), 1)

        def yscores(s, g):
            if g == 0:
                pe.wait_ge(sem("y_qk", s), 4)
                pe.wait_ge(sem("y_mask", s), 1)
            if g < 2:
                pe.wait_ge(sem("y_v8", s), g + 1)
            else:
                pe.wait_ge(sem("y_e", s), g - 1)
            mmul(bank(s, g % 2).rearrange("p (a b) -> p a b", a=4), ident_bf[:],
                 every(madd[s][:], 4), start=True, stop=False, skip_group_check=True)
            for j in range(4):
                h = y_head(g, j)
                r = slice(64 * (h % 2), 64 * (h % 2) + 64)
                mm = mmul(bank(s, g % 2, 128 * j, 128), q8[s][r, h // 2], k8[s][r, h // 2],
                          start=False, stop=True, skip_group_check=True)
            mm.then_inc(sem("y_s", s), 1)

        for s in lanes:
            yscores(s, 0)
        for g in range(4):
            for s in lanes:
                if g < 3:
                    yscores(s, g + 1)
            for s in lanes:
                pe.wait_ge(sem("y_p", s), g + 1)
                if g:
                    pe.wait_ge(sem("y_pT", s), g)
                for j in range(4):
                    mm = turned(bank(s, 2, 128 * j, 128), pe_[s][g % 2][:, j])
                mm.then_inc(sem("y_pT_ps", s), 1)
            for s in lanes:
                pe.wait_ge(sem("y_pT", s), g + 1)
                if g:
                    pe.wait_ge(sem("y_o8", s), g)
                for j in range(4):
                    h = y_head(g, j)
                    c = 256 * (g % 2) + 64 * j
                    for m in range(2):
                        mm = one(PS[s][64 * m:64 * m + 64, 3, c:c + 64],
                                 v8[s][:, h // 8, 64 * (h % 8):64 * (h % 8) + 64], pT[s][g % 2][:, j, m::2])
                mm.then_inc(sem("y_pv", s), 1)
        for s in lanes:
            pe.wait_ge(sem("y_o8", s), 4)
            for t in range(8):
                mm = mmul(bank(s, 2, 128, D), o8[s][:].rearrange("p a b -> p (a b)")[:, t::8], w("y_p", 128 * t, 128),
                          start=(t == 0), stop=(t == 7))
            mm.then_inc(sem("sub", s), 1)
        for s in lanes:
            ln_turn(s, 5)

        for s in lanes:
            pe.wait_ge(sem("xT", s), 5)
            for c in range(4):
                mm = one(bank(s, 1, 128 * c, 128), F1[:, 128 * c:128 * c + 128], xTs[s][:])
            mm.then_inc(sem("f_h_ps", s), 1)
        for s in lanes:
            pe.wait_ge(sem("f_g", s), 1)
            for c in range(4):
                mm = mmul(bank(s, 2, 128, D), hT[s][1][:, c], F2[:, c], start=(c == 0), stop=(c == 3))
            mm.then_inc(sem("sub", s), 1)

    @block.scalar
    def _(act):
        copy = nc.scalar.copy

        def tail(s, n):
            copy(oT[s][:].rearrange("p g q -> p (g q)"), bank(s, 3)).then_inc(sem("oT", s), 1)

        def tail_zT(s, n):
            act.wait_ge(sem("zT_ps", s), n)
            copy(zT[s][:], bank(s, 2, 0, 128)).then_inc(sem("zT", s), 1)

        def ln_T(s, n):
            act.wait_ge(sem("ln_T_ps", s), n)
            copy(xTs[s][:], bank(s, 0, 0, 128)).then_inc(sem("xT", s), 1)

        if part == "nystrom":
            for s in lanes:
                act.wait_ge(sem("n_proj", s), 1)
                copy(q4[s][:].rearrange("p g t -> p (g t)"), bank(s, 0)).then_inc(sem("n_qk", s), 1)
                act.wait_ge(sem("n_proj", s), 2)
                copy(kk[s][:, :, M:M + 128], bank(s, 1).rearrange("p (g t) -> p g t", g=TG)).then_inc(sem("n_qk", s), 1)
            for s in lanes:
                for j in range(TJ):
                    act.wait_ge(sem("n_s1", s), j + 1)
                    v = e1[s][:, j:H:TJ]
                    nc.scalar.activation(v, v, ACT.Exp, scale=0.5 * SC8).then_inc(sem("n_e1", s), 1)
            for half in range(2):
                for s in lanes:
                    act.wait_ge(sem("n_s23", s), 2 * half + 2)
                    v = p2[s][:, 4 * half:4 * half + 4]
                    nc.scalar.activation(v, v, ACT.Exp, scale=0.25 * SC8).then_inc(sem("n_e2", s), 1)
                    v = e3[s][:, 4 * half:4 * half + 4]
                    nc.scalar.activation(v, v, ACT.Exp, scale=0.5 * SC8).then_inc(sem("n_e23", s), 1)
            for s in lanes:
                act.wait_ge(sem("n_k2T_ps", s), 2)
                copy(k2T[s][:].rearrange("p a b -> p (a b)"), bank(s, 1)).then_inc(sem("n_k2T", s), 1)
            for s in lanes:
                for half in range(2):
                    act.wait_ge(sem("n_e3T_ps", s), half + 1)
                    copy(e3T[s][:, 4 * half:4 * half + 4].rearrange("p a b -> p (a b)"), bank(s, 2 + half)).then_inc(sem("n_e3T", s), 1)
            for s in lanes:
                for half in range(2):
                    act.wait_ge(sem("n_e1T_ps", s), half + 1)
                    copy(e1T[s][:, 4 * half:4 * half + 4].rearrange("p a b -> p (a b)"), bank(s, 2 + half)).then_inc(sem("n_e1T", s), 1)
            for k in range(NEWTON):
                for g in range(2):
                    for s in lanes:
                        act.wait_ge(sem("n_S_ps", s), 2 * k + g + 1)
                        copy(ss[s][g][:].rearrange("p a b -> p (a b)"), PS[s][:, g, 0:288]).then_inc(sem("n_S", s), 1)
                if k < NEWTON - 1:
                    for g in range(2):
                        for s in lanes:
                            act.wait_ge(sem("n_SW", s), 2 * k + g + 1)
                            nc.scalar.mul(ey[s][g][:].rearrange("p a b -> p (a b)"), PS[s][:, 2 + g, 0:288],
                                          0.25).then_inc(sem("n_e", s), 1)
            for s in lanes:
                act.wait_ge(sem("o_ps", s), 1)
                tail(s, 1)
            for s in lanes:
                tail_zT(s, 1)
            for s in lanes:
                ln_T(s, 1)

            return

        def attention8(n_att, plain, n_ln):
            if plain:
                for s in lanes:
                    act.wait_ge(sem("a_proj", s), 3 * (n_att - 1) + 1)
                    copy(q4[s][:].rearrange("p g t -> p (g t)"), bank(s, 0)).then_inc(sem("a_qk", s), 1)
                    act.wait_ge(sem("a_proj", s), 3 * (n_att - 1) + 2)
                    copy(kk[s][:, :, M:M + 128], bank(s, 1).rearrange("p (g t) -> p g t", g=TG)).then_inc(sem("a_qk", s), 1)
            for g in range(TG):
                for s in lanes:
                    n = 4 * (n_att - 1) + g
                    act.wait_ge(sem("a_nb", s), n + 1)
                    if g >= 2:
                        act.wait_ge(sem("a_pT_ps", s), n - 1)
                    for j in range(TJ):
                        ins = nc.scalar.activation(pe_[s][g % 2][:, j], bank(s, g % 2, 128 * j, 128), ACT.Exp,
                                                   bias=sm(s, "nb", 4 * g + j, 1), scale=SC8)
                    ins.then_inc(sem("a_p", s), 1)
            for s in lanes:
                act.wait_ge(sem("a_pv", s), 4 * n_att)
                tail(s, 1 + n_att)
            for s in lanes:
                tail_zT(s, 1 + n_att)
            for s in lanes:
                ln_T(s, n_ln)

        attention8(1, False, 2)
        for s in lanes:
            act.wait_ge(sem("m_pnb", s), 1)
            nc.scalar.activation(sm(s, "e8"), sm(s, "lg"), ACT.Exp, bias=sm(s, "pnb"),
                                 accum_out=sm(s, "psum")).then_inc(sem("m_e8", s), 1)
        for t in range(4):
            for s in lanes:
                if t % 2:
                    continue
                act.wait_ge(sem("m_h_ps", s), t + 1)
                if t >= 2:
                    act.wait_ge(sem("m_y", s), t - 1)
                for c in range(4):
                    ins = nc.scalar.activation(hT[s][t % 2][:, c], bank(s, t % 2, 128 * c, 128), ACT.Relu,
                                               bias=w("m_b1", 4 * t + c, 1))
                ins.then_inc(sem("m_h0", s), 1)
            if t == 0:
                for s in lanes:
                    act.wait_ge(sem("m_gT_ps", s), 1)
                    copy(gT[s][:], PS[s][0:EXPERTS, 3, 128:256]).then_inc(sem("m_gT", s), 1)
        for s in lanes:
            ln_T(s, 3)
        attention8(2, True, 4)
        for g in range(4):
            for s in lanes:
                act.wait_ge(sem("y_nb", s), g + 1)
                if g >= 2:
                    act.wait_ge(sem("y_pT_ps", s), g - 1)
                for j in range(4):
                    ins = nc.scalar.activation(pe_[s][g % 2][:, j], bank(s, g % 2, 128 * j, 128), ACT.Exp,
                                               bias=sm(s, "nb", 4 * g + j, 1), scale=SC64,
                                               accum_out=sm(s, "rs", 4 * g + j, 1))
                ins.then_inc(sem("y_e", s), 1)
            if g:
                for s in lanes:
                    y_o8(nc, act, sem, s, g - 1, o8, PS)
        for s in lanes:
            y_o8(nc, act, sem, s, 3, o8, PS)
        for s in lanes:
            ln_T(s, 5)
        for s in lanes:
            act.wait_ge(sem("f_h_ps", s), 1)
            copy(hT[s][0][:].rearrange("p a b -> p (a b)"), bank(s, 1)).then_inc(sem("f_h", s), 1)
        for s in lanes:
            act.wait_ge(sem("f_u", s), 1)
            nc.scalar.activation(hT[s][1][:], hT[s][1][:], ACT.Tanh, scale=GELU_C).then_inc(sem("f_t", s), 1)

    @block.gpsimd
    def _(pool):
        def rstd(s, n):
            pool.wait_ge(sem("ln_ve", s), n)
            nc.gpsimd.tensor_tensor(sm(s, "rstd"), sm(s, "ve"), w("mhalf"), ALU.pow).then_inc(sem("ln_rstd", s), 1)

        if part == "nystrom":
            for s in lanes:
                rstd(s, 1)
            return

        for s in lanes:
            rstd(s, 2)
        for s in lanes:
            rstd(s, 3)
        for s in lanes:
            pool.wait_ge(sem("ln_rows", s), 3)
            nc.gpsimd.tensor_tensor(xbo[s][:], xs[s][:], row("c_bo"), ALU.add).then_inc(sem("xbo", s), 1)
        for s in lanes:
            rstd(s, 4)
        for s in lanes:
            pool.wait_ge(sem("y_cve", s), 1)
            nc.gpsimd.tensor_tensor(sm(s, "crstd"), sm(s, "cve"), w("mhalf"), ALU.pow).then_inc(sem("y_crstd", s), 1)
            rstd(s, 5)
            pool.wait_ge(sem("ln_rows", s), 4)
            nc.gpsimd.tensor_tensor(xbo[s][:], xs[s][:], row("y_bo"), ALU.add).then_inc(sem("xbo", s), 1)
        for g in range(4):
            for s in lanes:
                pool.wait_ge(sem("y_rs", s), g + 1)
                v = pe_[s][g % 2][:]
                nc.gpsimd.tensor_tensor(v, v, over(sm(s, "rs", 4 * g, 4), 128), ALU.mult).then_inc(sem("y_p", s), 1)
        for s in lanes:
            rstd(s, 6)
        for s in lanes:
            rstd(s, 7)

    @block.vector
    def _(dve):
        V = nc.vector
        count = [0]
        steps = "n_vector_steps" if part == "nystrom" else "vector_steps"

        def link(ins):
            count[0] += 1
            ins.then_inc(sem(steps), 1)
            dve.wait_ge(sem(steps), count[0])

        def stats(s, src, st, mv, ve):
            link(V.bn_stats(sm(s, st), src))
            link(V.bn_aggr(sm(s, mv), sm(s, st)))
            return V.tensor_scalar(sm(s, ve), sm(s, mv, 1, 1), EPS, None, ALU.add)

        def ln_stats(s, n, residual):
            dve.wait_ge(sem("sub", s), n)
            link(V.tensor_tensor(res[s][:], bank(s, 2, 128, D), residual, ALU.add))

        def ln_rows(s, n, n_rstd):
            dve.wait_ge(sem("ln_rstd", s), n_rstd)
            V.tensor_scalar(xs[s][:], res[s][:], sm(s, "mv", 0, 1), sm(s, "rstd"),
                            ALU.subtract, ALU.mult).then_inc(sem("ln_rows", s), 1)

        def tail(s, n):
            dve.wait_ge(sem("o_rows", s), n)
            v = bank(s, 0).rearrange("p (h e) -> p h e", e=TW)
            link(V.reciprocal(sm(s, "rs"), v[:, :, HD]))
            dst = z[s][:] if n == 1 else z[s][:].rearrange("p (i g) e -> p g i e", i=TG)
            r = over(sm(s, "rs"), HD)
            a = v[:, :, 0:HD]
            if n > 1:
                r, a = (t.rearrange("p (g i) e -> p g i e", g=TJ) for t in (r, a))
            V.tensor_tensor(dst, a, r, ALU.mult).then_inc(sem("z", s), 1)

        if part == "nystrom":
            for s in lanes:
                for t in range(2):
                    dve.wait_ge(sem("n_qk", s), t + 1)
                    src = q4[s][:] if t == 0 else kk[s][:, :, M:M + 128]
                    dst = ql[s][:] if t == 0 else kk[s][:, :, 0:M]
                    V.tensor_tensor(dst, src[:, :, 0:128:2], src[:, :, 1:128:2], ALU.add).then_inc(sem("n_lm", s), 1)
                dve.wait_ge(sem("n_proj", s), 3)
                V.tensor_copy(v9[s][:, :, 0:HD], bank(s, 2, 0, D).rearrange("p (h e) -> p h e", e=HD)).then_inc(sem("n_v9", s), 1)

            def s1(s, j):
                dve.wait_ge(sem("n_k1", s), j + 1)
                v = bank(s, j % 2, 0, 256).rearrange("p (h m) -> p h m", m=M)
                link(V.tensor_reduce(sm(s, "mx1", 4 * j, 4), v, AX, ALU.max))
                V.tensor_tensor(e1[s][:, j:H:TJ], v, over(sm(s, "mx1", 4 * j, 4), M), ALU.subtract).then_inc(sem("n_s1", s), 1)

            def s23(s, t):
                dve.wait_ge(sem("n_k23", s), t + 1)
                v = PS[s][:, 2 + t % 2, 0:384].rearrange("p (a b) -> p a b", a=2)
                V.tensor_reduce(sm(s, "mx2", 2 * t, 2), v[:, :, 0:M], AX, ALU.max)
                link(V.tensor_reduce(sm(s, "mx3", 2 * t, 2), v[:, :, M:192], AX, ALU.max))
                V.tensor_tensor(p2[s][:, quarter(t)], v[:, :, 0:M], over(sm(s, "mx2", 2 * t, 2), M), ALU.subtract)
                V.tensor_tensor(e3[s][:, quarter(t)], v[:, :, M:192], over(sm(s, "mx3", 2 * t, 2), 128),
                                ALU.subtract).then_inc(sem("n_s23", s), 1)

            for s in lanes:
                for j in range(2):
                    s1(s, j)
                for t in range(2):
                    s23(s, t)
            for j in range(2, TJ):
                for s in lanes:
                    s1(s, j)
            for t in range(2, 4):
                for s in lanes:
                    s23(s, t)
            for half in range(2):
                for s in lanes:
                    dve.wait_ge(sem("n_e2", s), half + 1)
                    v = p2[s][:, 4 * half:4 * half + 4]
                    r = sm(s, "rs2", 4 * half, 4)
                    link(V.tensor_reduce(r, v, AX, ALU.add))
                    link(V.reciprocal(r, r))
                    V.tensor_tensor(v, v, over(r, M), ALU.mult).then_inc(sem("n_p2", s), 1)
            for s in lanes:
                dve.wait_ge(sem("n_colsum", s), 2)
                link(V.tensor_reduce(sm(s, "rd"), bank(s, 0).rearrange("p (a b) -> p a b", b=M), AX, ALU.max))
                link(V.reciprocal(sm(s, "rd"), sm(s, "rd")))
                V.tensor_scalar(sm(s, "mx2"), sm(s, "rd"), -1.0, None, ALU.mult).then_inc(sem("n_rd", s), 1)
                dve.wait_ge(sem("n_rd", s), 1)
            for s in lanes:
                for g in range(2):
                    dve.wait_ge(sem("n_kkT", s), g + 1)
                    v = PS[s][:, g, 0:288].rearrange("p (a b) -> p a b", a=4)[:, :, 0:M]
                    E = ey[s][g][:, :, 0:M]
                    link(V.tensor_tensor(E, v, over(sm(s, "mx2")[:, g:PAIRS:2], M), ALU.mult))
                    V.tensor_tensor(E, E, every(w("ident2"), 4), ALU.add).then_inc(sem("n_e", s), 1)
                dve.wait_ge(sem("n_y0", s), 1)
                v = bank(s, 2, 0, 128).rearrange("p (a b) -> p a b", b=16)
                link(V.reciprocal(sm(s, "rs3"), v[:, :, HD]))
                for g in range(2):
                    V.tensor_tensor(ey[s][g][:, :, M:M + HD], v[:, g:PAIRS:2, 0:HD],
                                    over(sm(s, "rs3")[:, g:PAIRS:2], HD), ALU.mult).then_inc(sem("n_y", s), 1)
            for k in range(NEWTON):
                for g in range(2):
                    for s in lanes:
                        dve.wait_ge(sem("n_S", s), 2 * k + g + 1)
                        v = ss[s][g][:]
                        Y = ey[s][g][:, :, M:M + HD]
                        V.tensor_tensor(uu[s][g][:], v[:, :, M:M + HD], Y, ALU.add)
                        ins = V.scalar_tensor_tensor(wz[s][g][:, :, M:M + HD], v[:, :, M:M + HD], 0.25, Y, ALU.mult, ALU.add)
                        if k < NEWTON - 1:
                            ins = V.scalar_tensor_tensor(wz[s][g][:, :, 0:M], ey[s][g][:, :, 0:M], 3.0, v[:, :, 0:M],
                                                         ALU.mult, ALU.add)
                        ins.then_inc(sem("n_wz", s), 1)
                for g in range(2):
                    for s in lanes:
                        Y = ey[s][g][:, :, M:M + HD]
                        if k < NEWTON - 1:
                            dve.wait_ge(sem("n_e", s), 2 * k + g + 3)
                            ins = V.scalar_tensor_tensor(Y, Y, 4.0, uu[s][g][:], ALU.mult, ALU.add)
                        else:
                            dve.wait_ge(sem("n_SW", s), 2 * k + g + 1)
                            v = PS[s][:, 2 + g, 0:288].rearrange("p (a b) -> p a b", a=4)
                            ins = V.tensor_tensor(Y, v[:, :, M:M + HD], uu[s][g][:], ALU.add)
                        ins.then_inc(sem("n_y", s), 1)
            for s in lanes:
                dve.wait_ge(sem("n_w_ps", s), 1)
                V.tensor_tensor(w9[s][:, :, 0:HD], bank(s, 0, 0, 128).rearrange("p (a b) -> p a b", b=16)[:, :, 0:HD],
                                over(sm(s, "rd"), HD), ALU.mult).then_inc(sem("n_w9", s), 1)
            for s in lanes:
                tail(s, 1)
            for s in lanes:
                dve.wait_ge(sem("x_in", s), 16)
                ln_stats(s, 1, xs[s][:])
                stats(s, res[s][:], "st", "mv", "ve").then_inc(sem("ln_ve", s), 1)
            for s in lanes:
                ln_rows(s, 1, 1)

            return

        def attention8(n_att, aug, residual, n_ln):
            for s in lanes:
                if aug:
                    dve.wait_ge(sem("a_proj", s), 1)
                    V.tensor_tensor(q4[s][:], bank(s, 0).rearrange("p (g t) -> p g t", g=TG), every(w("qaug"), TG),
                                    ALU.add).then_inc(sem("a_qk", s), 1)
                    dve.wait_ge(sem("a_proj", s), 2)
                    V.tensor_tensor(kk[s][:, :, M:M + 128], bank(s, 1).rearrange("p (g t) -> p g t", g=TG),
                                    o["kaug"][:], ALU.add).then_inc(sem("a_qk", s), 1)
                dve.wait_ge(sem("a_proj", s), 3 * n_att)
                V.tensor_copy(v9[s][:, :, 0:HD], bank(s, 2, 0, D).rearrange("p (h e) -> p h e", e=HD)).then_inc(sem("a_v9", s), 1)

            def mx(s, g):
                dve.wait_ge(sem("a_s", s), 4 * (n_att - 1) + g + 1)
                link(V.tensor_reduce(sm(s, "mx", 4 * g, 4), bank(s, g % 2).rearrange("p (a b) -> p a b", a=4), AX, ALU.max))
                V.tensor_scalar(sm(s, "nb", 4 * g, 4), sm(s, "mx", 4 * g, 4), -SC8, None, ALU.mult).then_inc(sem("a_nb", s), 1)

            for s in lanes:
                mx(s, 0)
            for g in range(TG):
                for s in lanes:
                    if g + 1 < TG:
                        mx(s, g + 1)
                for s in lanes:
                    n = 4 * (n_att - 1) + g
                    dve.wait_ge(sem("a_pT_ps", s), n + 1)
                    if g >= 2:
                        dve.wait_ge(sem("a_pv", s), n - 1)
                    V.tensor_copy(pT[s][g % 2][:].rearrange("p a b -> p (a b)"), bank(s, 2)).then_inc(sem("a_pT", s), 1)
            for s in lanes:
                tail(s, 1 + n_att)
            for s in lanes:
                ln_stats(s, n_ln - (n_ln > 3), residual(s))
                stats(s, res[s][:], "st", "mv", "ve").then_inc(sem("ln_ve", s), 1)
            for s in lanes:
                ln_rows(s, n_ln, n_ln)

        attention8(1, True, lambda s: xs[s][:], 2)

        for s in lanes:
            dve.wait_ge(sem("m_logits", s), 1)
            link(V.tensor_tensor(sm(s, "lg"), bank(s, 3, 0, EXPERTS), row("m_br"), ALU.add))
            link(V.tensor_reduce(sm(s, "pmx"), sm(s, "lg"), AX, ALU.max))
            V.tensor_scalar(sm(s, "pnb"), sm(s, "pmx"), -1.0, None, ALU.mult).then_inc(sem("m_pnb", s), 1)
        for s in lanes:
            dve.wait_ge(sem("m_e8", s), 1)
            link(V.tensor_reduce(sm(s, "emx"), sm(s, "e8"), AX, ALU.max))
            V.reciprocal(sm(s, "grs"), sm(s, "psum"))
            link(V.tensor_scalar(sm(s, "gate"), sm(s, "e8"), sm(s, "emx"), None, ALU.is_ge))
            link(V.tensor_tensor(sm(s, "gate"), sm(s, "gate"), w("first"), ALU.mult))
            link(V.tensor_reduce(sm(s, "fmx"), sm(s, "gate"), AX, ALU.max))
            link(V.tensor_tensor(sm(s, "gp"), sm(s, "emx"), sm(s, "grs"), ALU.mult))
            V.tensor_scalar(sm(s, "gate"), sm(s, "gate"), sm(s, "fmx"), sm(s, "gp"), ALU.is_ge, ALU.mult
                            ).then_inc(sem("m_gate", s), 1)

        def relu(s, t):
            dve.wait_ge(sem("m_h_ps", s), t + 1)
            if t >= 2:
                dve.wait_ge(sem("m_y", s), t - 1)
            for c in range(4):
                ins = V.tensor_scalar(hT[s][t % 2][:, c], bank(s, t % 2, 128 * c, 128), w("m_b1", 4 * t + c, 1), 0.0,
                                      ALU.add, ALU.max)
            ins.then_inc(sem("m_h1", s), 1)

        for t in range(4):
            for s in lanes:
                if t % 2 == 0:
                    relu(s, t + 1)
            if t == 0:
                for s in lanes:
                    dve.wait_ge(sem("m_b2", s), 1)
                    V.tensor_tensor(res[s][:], bank(s, 3, 256, D), xs[s][:], ALU.add).then_inc(sem("m_res", s), 1)
                    dve.wait_ge(sem("m_res", s), 1)
            for s in lanes:
                dve.wait_ge(sem("m_y", s), t + 1)
                for e in (2 * t, 2 * t + 1):
                    V.scalar_tensor_tensor(res[s][:], bank(s, 2 + t % 2, 128 * (e % 2), 128), sm(s, "gate", e, 1), res[s][:],
                                           ALU.mult, ALU.add).then_inc(sem("m_y_used", s), 1)
                    dve.wait_ge(sem("m_y_used", s), e + 1)
        for s in lanes:
            stats(s, res[s][:], "st", "mv", "ve").then_inc(sem("ln_ve", s), 1)
        for s in lanes:
            ln_rows(s, 3, 3)

        def xbo_of(s):
            dve.wait_ge(sem("xbo", s), 1)
            return xbo[s][:]

        attention8(2, False, xbo_of, 4)

        for s in lanes:
            stats(s, cs[s][:], "cst", "cmv", "cve").then_inc(sem("y_cve", s), 1)
            V.tensor_scalar(madd[s][:], ms[s][:], 0.0, NEG, ALU.is_equal, ALU.mult).then_inc(sem("y_mask", s), 1)
            dve.wait_ge(sem("ln_rows", s), 4)
            stats(s, xs[s][:], "st", "mv", "ve").then_inc(sem("ln_ve", s), 1)
            dve.wait_ge(sem("y_crstd", s), 1)
            V.tensor_scalar(cn[s][:], cs[s][:], sm(s, "cmv", 0, 1), sm(s, "crstd"), ALU.subtract, ALU.mult
                            ).then_inc(sem("y_cn", s), 1)
            dve.wait_ge(sem("ln_rstd", s), 5)
            V.tensor_scalar(xn[s][:], xs[s][:], sm(s, "mv", 0, 1), sm(s, "rstd"), ALU.subtract, ALU.mult
                            ).then_inc(sem("y_xn", s), 1)
        for s in lanes:
            dve.wait_ge(sem("y_cnT_ps", s), 1)
            dve.wait_ge(sem("y_xnT_ps", s), 1)
            V.tensor_scalar(cnT[s][:], bank(s, 1, 0, 128), w("y_g"), w("y_b"), ALU.mult, ALU.add).then_inc(sem("y_T", s), 1)
            V.tensor_scalar(xnT[s][:], bank(s, 1, 128, 128), w("y_g"), w("y_b"), ALU.mult, ALU.add).then_inc(sem("y_T", s), 1)
        for s in lanes:
            for b, (dst, bias) in enumerate(((q8, "y_bq"), (q8, "y_bq"), (k8, "y_bk"), (k8, "y_bk"))):
                dve.wait_ge(sem("y_qk_ps", s), b + 1)
                c = 4 * (b % 2)
                V.tensor_tensor(dst[s][:, c:c + 4], bank(s, b).rearrange("p (a b) -> p a b", a=4),
                                over(w(bias, c, 4), 128), ALU.add).then_inc(sem("y_qk", s), 1)
        for s in lanes:
            for b in range(2):
                dve.wait_ge(sem("y_v_ps", s), b + 1)
                V.tensor_tensor(v8[s][:, b], bank(s, b), row("y_bv")[:, 512 * b:512 * b + 512], ALU.add).then_inc(sem("y_v8", s), 1)

        def ymax(s, g):
            dve.wait_ge(sem("y_s", s), g + 1)
            link(V.tensor_reduce(sm(s, "mx", 4 * g, 4), bank(s, g % 2).rearrange("p (a b) -> p a b", a=4), AX, ALU.max))
            V.tensor_scalar(sm(s, "nb", 4 * g, 4), sm(s, "mx", 4 * g, 4), -SC64, None, ALU.mult).then_inc(sem("y_nb", s), 1)

        for s in lanes:
            ymax(s, 0)
        for g in range(4):
            for s in lanes:
                dve.wait_ge(sem("y_e", s), g + 1)
                r = sm(s, "rs", 4 * g, 4)
                V.reciprocal(r, r).then_inc(sem("y_rs", s), 1)
            for s in lanes:
                if g < 3:
                    ymax(s, g + 1)
            for s in lanes:
                dve.wait_ge(sem("y_pT_ps", s), g + 1)
                if g >= 2:
                    dve.wait_ge(sem("y_pv", s), g - 1)
                V.tensor_copy(pT[s][g % 2][:].rearrange("p a b -> p (a b)"), bank(s, 2)).then_inc(sem("y_pT", s), 1)
        for s in lanes:
            dve.wait_ge(sem("xbo", s), 2)
            ln_stats(s, 4, xbo[s][:])
            stats(s, res[s][:], "st", "mv", "ve").then_inc(sem("ln_ve", s), 1)
        for s in lanes:
            ln_rows(s, 5, 6)

        for s in lanes:
            dve.wait_ge(sem("f_h", s), 1)
            h, u = hT[s][0][:], hT[s][1][:]
            link(V.tensor_tensor(u, h, h, ALU.mult))
            link(V.tensor_scalar(u, u, GELU_A, 1.0, ALU.mult, ALU.add))
            V.tensor_tensor(u, u, h, ALU.mult).then_inc(sem("f_u", s), 1)
        for s in lanes:
            dve.wait_ge(sem("f_t", s), 1)
            h, u = hT[s][0][:], hT[s][1][:]
            V.scalar_tensor_tensor(u, u, 1.0, h, ALU.add, ALU.mult).then_inc(sem("f_g", s), 1)
        for s in lanes:
            ln_stats(s, 5, xs[s][:])
            stats(s, res[s][:], "st", "mv", "ve").then_inc(sem("ln_ve", s), 1)
        for s in lanes:
            ln_rows(s, 6, 7)


def n_k1(nc, sem, s, j, PS, q4, kk):
    r = slice(TW * j, TW * j + TW)
    for g in range(TG):
        mm = nc.tensor.matmul(PS[s][:, j % 2, M * g:M * g + M], q4[s][r, g], kk[s][r, g, 0:M], start=True, stop=True)
    mm.then_inc(sem("n_k1", s), 1)


def quarter(t):
    p = 4 * (t // 2) + t % 2
    return slice(p, p + 3, 2)


def n_k23(nc, sem, s, t, PS, ql, kk):
    for c in range(2):
        for m in range(2):
            j = 2 * (t % 2) + m
            r = slice(TW * j, TW * j + TW)
            g = 2 * (t // 2) + c
            mm = nc.tensor.matmul(PS[s][M * m:M * m + M, 2 + t % 2, 192 * c:192 * c + 192], ql[s][r, g], kk[s][r, g],
                                  start=True, stop=True)
    mm.then_inc(sem("n_k23", s), 1)


def y_o8(nc, act, sem, s, g, o8, PS):
    act.wait_ge(sem("y_pv", s), g + 1)
    h = y_head(g, 0)
    nc.scalar.copy(o8[s][:].rearrange("p a (b c) -> p (a b) c", c=M)[:, h:h + 7:2],
                   PS[s][:, 3, 256 * (g % 2):256 * (g % 2) + 256].rearrange("p (a b) -> p a b", a=4)
                   ).then_inc(sem("y_o8", s), 1)


def y_head(g, j):
    return 2 * (4 * (g // 2) + j) + g % 2


def kernel(**inputs):
    import concourse.bacc as bacc
    from concourse.bass_utils import run_bass_kernel_spmd

    a = {k: np.asarray(v) for k, v in inputs.items()}

    def tiles4(m):
        t = np.zeros((D, H, TW), m.dtype)
        t[:, :, :HD] = m.reshape(D, H, HD)
        return t.reshape(D, H * TW)

    qkv = a["L0_attn_w_qkv"]
    kv = a["L0_xattn_w_kv"]
    part = {
        "n_q4": tiles4(qkv[:, :D]), "n_k4": tiles4(qkv[:, D:2 * D]), "n_v": qkv[:, 2 * D:], "n_p": a["L0_attn_w_proj"],
        "x_q4": tiles4(a["L0_xattn_w_q"]), "x_k4": tiles4(kv[:, :D]), "x_v": kv[:, D:], "x_p": a["L0_xattn_w_proj"],
        "c_q4": tiles4(a["L1_attn_Wq"].T), "c_k4": tiles4(a["L1_attn_Wk"].T), "c_v": a["L1_attn_Wv"].T,
        "c_p": a["L1_attn_Wo"].T,
        "m_r": a["L0_ffn_Wr"], "m_1": a["L0_ffn_W1"].transpose(1, 0, 2).reshape(D, -1),
        "m_2": a["L0_ffn_W2"].reshape(16, 128, D).transpose(1, 0, 2).reshape(128, -1),
        "y_q": a["L1_xattn_Wq"], "y_k": a["L1_xattn_Wk"], "y_v": a["L1_xattn_Wv"],
        "y_p": a["L1_xattn_Wo"].reshape(8, 128, D).transpose(1, 0, 2).reshape(128, -1),
        "m_b1": a["L0_ffn_b1"].reshape(16, 128).T, "y_bq": a["L1_xattn_bq"].reshape(8, 128).T,
        "y_bk": a["L1_xattn_bk"].reshape(8, 128).T, "y_g": a["L1_xattn_gamma"][:, None],
        "y_b": a["L1_xattn_beta"][:, None],
        "x_rel": np.repeat(a["L0_xattn_w_rel"].reshape(TG, TJ).T, TW, axis=0),
    }
    f = np.float32
    part["ident"] = np.eye(128, dtype=f)
    part["ones2"] = np.kron(np.eye(2, dtype=f), np.ones((M, M), f))
    part["ident2"] = np.tile(np.eye(M, dtype=f), (2, 1))
    pos, at = np.arange(128, dtype=f), np.arange(128) % TW
    part["qaug"] = np.where(at[:, None] == HD, pos[None], np.where(at[:, None] == HD + 1, -1, 0)).astype(f)
    part["kpat"] = ((at == HD) | (at == HD + 1)).astype(f)[:, None] * np.ones((1, 128), f)
    part["kpos"] = np.where(at[:, None] == HD + 1, pos[None], 1).astype(f)
    part["causal"] = np.triu(np.full((128, 128), -1e30, f), 1)
    part["first"] = np.tile(EXPERTS - np.arange(EXPERTS, dtype=f), (128, 1))
    part["mhalf"] = np.full((128, 1), -0.5, f)
    wpack = np.concatenate([part[n] for n, _ in WEIGHTS], axis=1)
    rows = np.concatenate([a["L0_ffn_br"], a["L1_attn_bo"], a["L1_xattn_bo"], a["L1_xattn_bv"],
                           a["L1_ffn_fc1_logits"], a["L1_ffn_fc2_logits"]])[None]

    def chunks(m):
        return m.reshape(16, 128, -1).transpose(1, 0, 2)

    arrays = {
        "x": a["x"], "xT": a["x"].transpose(0, 2, 1), "ctx": a["ctx_1024"], "ctxT": a["ctx_1024"].transpose(0, 2, 1),
        "mask": a["mask_Bx1xSxS2_ik1"].reshape(B, S, S), "wpack": wpack, "rows": rows, "b2": a["L0_ffn_b2"],
        "a1": chunks(a["L1_ffn_fc1_A"].transpose(0, 2, 1)), "b1": chunks(a["L1_ffn_fc1_B"]),
        "a2": chunks(a["L1_ffn_fc2_A"].transpose(0, 2, 1)), "b2w": chunks(a["L1_ffn_fc2_B"]),
    }
    arrays = {f"in_{k}": np.ascontiguousarray(v) for k, v in arrays.items()}
    nc = bacc.Bacc("TRN2", target_bir_lowering=False, num_devices=1)
    args = [nc.dram_tensor(k, v.shape, mybir.dt.from_np(v.dtype), kind="ExternalInput").ap() for k, v in arrays.items()]
    out = nc.dram_tensor("out", (B, S, D), F32, kind="ExternalOutput").ap()
    build(nc, *args, out)
    r = run_bass_kernel_spmd(nc, [arrays], core_ids=[0])
    return r.results[0]["out"]
```

```python
from contextlib import ExitStack

import numpy as np

import concourse.bass as bass
from concourse import mybir

F32 = mybir.dt.float32
BF16 = mybir.dt.bfloat16
I32 = mybir.dt.int32
ALU = mybir.AluOpType
ACT = mybir.ActivationFunctionType
AX = mybir.AxisListType.X

B, S, D = 32, 128, 128
LANES = 2
H, HD = 16, 8
TG, TJ, TW = 4, 4, 32
M = 64
PAIRS = H // 2
NEWTON = 6
PW = 2 * M + HD
GROUPS = ((0, 3), (3, 6), (6, 8))
EXPERTS, HID = 8, 256
XH, XHD = 16, 64
PRIM, RANK, FF = 32, 64, 512
EPS = 1e-5
SC8 = float(HD) ** -0.5
SC64 = float(XHD) ** -0.5
NEG = -1e20
GELU_C, GELU_A = 0.7978845608028654, 0.044715

WEIGHTS = [
    ("n_q", D), ("n_k", D), ("n_v", D), ("n_p", D),
    ("x_q4", 512), ("x_k4", 512), ("x_v", D), ("x_p", D),
    ("c_q", D), ("c_k", D), ("c_v", D), ("c_p", D),
    ("m_r", EXPERTS), ("m_1", EXPERTS * HID), ("m_2", EXPERTS * HID),
    ("y_q", XH * XHD), ("y_k", XH * XHD), ("y_v", XH * XHD), ("y_p", XH * XHD),
    ("m_b1", 16), ("y_bq", 8), ("y_bk", 8), ("y_g", 1), ("y_b", 1), ("x_rel", TG),
    ("ident", 128), ("ones2", 128), ("ident2", M), ("qaug", 128), ("kpat", 128), ("kpos", 128),
    ("causal", 128), ("first", EXPERTS), ("mhalf", 1), ("gmask", TG), ("hmask", TJ), ("mask16", H),
]
WCOL = {}
for _n, _w in WEIGHTS:
    WCOL[_n] = (sum(w for _, w in WEIGHTS[:len(WCOL)]), _w)
NW = sum(w for _, w in WEIGHTS)
ROWS = [("m_br", EXPERTS), ("c_bo", D), ("y_bo", D), ("y_bv", XH * XHD), ("l1", PRIM), ("l2", PRIM)]
RCOL = {}
for _n, _w in ROWS:
    RCOL[_n] = (sum(w for _, w in ROWS[:len(RCOL)]), _w)
NR = sum(w for _, w in ROWS)


def slots(*parts):
    flat, at = [item for part in parts for item in part], 0
    total, out = sum(n for _, n in flat), []
    for name, n in flat:
        out.append((at / total, name))
        at += n
    return out


def attention_slots(n_att, n_ln):
    a = f"r{n_att}"
    return [(f"{a}.proj", 22), (f"{a}.first", 10)] + [x for g in range(4) for x in ((f"{a}.s{g}", 15), (f"{a}.t{g}", 12))] + [
        (f"{a}.last", 8), (f"{a}.rows", 10), (f"{a}.z", 8), (f"{a}.out", 15), (f"r.ln{n_ln}", 15)]


LAG = {"n": 0.03, "r": 0.001}
N_SLOTS = slots(
    [("n.proj", 20), ("n.s0", 22), ("n.s1", 22), ("n.col0", 9), ("n.col1", 9), ("n.e3T", 9), ("n.e1T", 9),
     ("n.kkT", 13), ("n.y0", 13)],
    [(f"n.{p}{k}{g}", 9) for k in range(NEWTON) for p in "SW" for g in range(len(GROUPS))],
    [("n.w", 13), ("n.o", 12), ("n.rows", 8), ("n.z", 8), ("n.out", 12), ("n.ln", 12)])
R_SLOTS = slots(
    attention_slots(1, 2),
    [("rm.first", 20)] + [x for t in range(4) for x in ((f"rm.h{t}", 13), (f"rm.y{t}", 13))] + [("r.ln3", 15)],
    attention_slots(2, 4),
    [("ry.stats", 15), ("ry.norm", 15), ("ry.T", 8), ("ry.q0", 10), ("ry.q1", 10), ("ry.first", 10)]
    + [x for g in range(4) for x in ((f"ry.s{g}", 18), (f"ry.t{g}", 12))] + [("ry.last", 10), ("ry.out", 25), ("r.ln5", 15)],
    [("rf.h", 20), ("rf.u", 15), ("rf.out", 20), ("rf.ln", 10)])


def build(nc, x, xT, ctx, ctxT, mask, wpack, rows, b2, a1, b1, a2, b2w, out):
    with ExitStack() as top:
        def sb(name, shape, dt=F32, scope=top):
            return scope.enter_context(nc.sbuf_tensor(name, shape, dt))

        W = sb("weights", [128, NW])
        R = sb("row_weights", [128, NR])
        b2s = sb("expert_b2", [EXPERTS, D])
        F1 = sb("ffn_w1", [128, FF])
        F2 = sb("ffn_w2", [128, 4, D])
        kaug = sb("kaug", [128, TG, 128])
        ident_bf = sb("ident_bf", [128, 128], BF16)
        causal_bf = sb("causal_bf", [128, 128], BF16)

        def w(name, a=0, n=None):
            c, width = WCOL[name]
            return W[:, c + a:c + a + (width - a if n is None else n)]

        def row(name):
            c, width = RCOL[name]
            return R[:, c:c + width]

        ident = w("ident")
        lanes = range(LANES)
        def lane(name, shape, dt=F32):
            return [sb(f"{name}{s}", shape, dt) for s in lanes]

        v9 = lane("v9", [128, H, TW])
        w9 = lane("w9", [128, PAIRS, TW])
        ey = lane("ey", [128, PAIRS, PW])
        xin = lane("x_in_rows", [128, D])
        xTin = lane("x_in_T", [128, 128])
        xs = lane("x_rows", [128, D])
        stored = [nc.alloc_semaphore(f"stored{s}") for s in lanes]
        PS = [top.enter_context(nc.psum_tensor(f"ps{s}", [128, 4, 512], F32)) for s in lanes]

        def sm(s, name, a=0, n=None):
            place = {"mx1": (0, 16), "mx2": (16, 8), "mx3": (24, 8), "rs2": (32, 8), "rd": (40, 8),
                     "rs3": (48, 8), "mx": (56, 16), "nb": (72, 16), "rs": (88, 16), "st": (104, 6),
                     "mv": (110, 2), "ve": (112, 1), "rstd": (113, 1), "cst": (114, 6), "cmv": (120, 2),
                     "cve": (122, 1), "crstd": (123, 1), "lg": (124, 8), "e8": (132, 8), "gate": (140, 8),
                     "pmx": (148, 1), "pnb": (149, 1), "psum": (150, 1), "emx": (151, 1), "fmx": (152, 1),
                     "grs": (153, 1), "gp": (154, 1), "nb1": (160, 16), "nb3": (176, 8)}
            c, width = place[name]
            return small[s][:, c + a:c + a + (width - a if n is None else n)]

        def over(ap, n):
            return ap.unsqueeze(2).to_broadcast([128, ap.shape[1], n])

        def every(ap, n):
            return ap.unsqueeze(1).to_broadcast([128, n, ap.shape[1]])

        with ExitStack() as pre:
            A1 = sb("fc1_A", [128, 16, D], scope=pre)
            B1 = sb("fc1_B", [128, 16, FF], scope=pre)
            A2 = sb("fc2_A", [128, 16, FF], scope=pre)
            B2 = sb("fc2_B", [128, 16, D], scope=pre)
            lw = sb("mix", [128, 2, PRIM], scope=pre)
            lcol = sb("mix_col", [128, 2, 16], scope=pre)
            tmp = sb("mix_tmp", [128, 8], scope=pre)

            pre_sems = []

            def sem(name):
                pre_sems.append(nc.alloc_semaphore(name))
                return pre_sems[-1]
            weights_in, rows_in = sem("weights_in"), sem("rows_in")
            fc_in = [sem(f"{name}_in") for name in ("fc1_A", "fc1_B", "fc2_B", "fc2_A")]
            steps, mixed, scaled, composed = sem("pre_steps"), sem("mixed"), sem("scaled"), sem("composed")
            mix_max, cleared = sem("mix_max"), sem("cleared")
            block = nc.Block()
            pre.enter_context(block)

            @block.sync
            def _(sp):
                sp.dma_start(R[:], rows.to_broadcast([128, NR])).then_inc(rows_in, 16)
                for n, (dst, src) in enumerate(((A1, a1), (B1, b1), (B2, b2w), (A2, a2))):
                    for half in range(2):
                        c = slice(8 * half, 8 * half + 8)
                        sp.dma_start(dst[:, c], src[:, c]).then_inc(fc_in[n], 16)
                for s in lanes:
                    sp.dma_start(xin[s][:], x[s]).then_inc(weights_in, 16)
                    sp.dma_start(xTin[s][:], xT[s]).then_inc(weights_in, 16)
                sp.dma_start(W[:], wpack).then_inc(weights_in, 16)
                sp.dma_start(b2s[:], b2).then_inc(weights_in, 16)
                sp.wait_ge(weights_in, 16 * (2 * LANES + 2))

            @block.scalar
            def _(act):
                act.wait_ge(mix_max, 1)
                for n in range(2):
                    nc.scalar.activation(lw[:, n], row(f"l{n + 1}"), ACT.Exp, bias=tmp[:, 2 + n:3 + n],
                                         accum_out=tmp[:, 4 + n:5 + n]).then_inc(mixed, 1)

            @block.vector
            def _(dve):
                count = [0]

                def link(ins):
                    count[0] += 1
                    ins.then_inc(steps, 1)
                    dve.wait_ge(steps, count[0])

                for s in lanes:
                    nc.vector.memset(ey[s][:], 0.0)
                    nc.vector.memset(v9[s][:], 0.0)
                    link(nc.vector.memset(w9[s][:], 0.0))
                    nc.vector.memset(v9[s][:, :, HD:HD + 1], 1.0)
                    link(nc.vector.memset(w9[s][:, :, HD:HD + 1], 1.0))
                    nc.vector.memset(xs[s][:], 0.0).then_inc(stored[s], 16)
                dve.wait_ge(rows_in, 16)
                for n in range(2):
                    nc.vector.tensor_reduce(tmp[:, n:n + 1], row(f"l{n + 1}"), AX, ALU.max).then_inc(cleared, 1)
                dve.wait_ge(cleared, 2)
                nc.vector.tensor_scalar(tmp[:, 2:4], tmp[:, 0:2], -1.0, None, ALU.mult).then_inc(mix_max, 1)
                dve.wait_ge(mixed, 2)
                link(nc.vector.reciprocal(tmp[:, 6:8], tmp[:, 4:6]))
                link(nc.vector.tensor_scalar(tmp[:, 7:8], tmp[:, 7:8], 0.5, None, ALU.mult))
                for n in range(2):
                    for half in range(2):
                        p = slice(64 * half, 64 * half + 64)
                        ins = nc.vector.tensor_scalar(lcol[p, n, :], lw[p, n, half:PRIM:2],
                                                      tmp[p, 6 + n:7 + n], None, ALU.mult)
                link(ins)
                for n, a in ((0, A1), (1, B2)):
                    dve.wait_ge(fc_in[2 * n], 32)
                    nc.vector.tensor_tensor(a[:], a[:], over(lcol[:, n], D), ALU.mult).then_inc(scaled, 1)
                dve.wait_ge(weights_in, 16 * (2 * LANES + 2))
                for g in range(TG):
                    link(nc.vector.tensor_tensor(kaug[:, g], w("kpat"), w("kpos"), ALU.mult))
                    link(nc.vector.tensor_scalar(kaug[:, g], kaug[:, g], w("x_rel", g, 1), 1.0 / SC8,
                                                 ALU.mult, ALU.mult))
                nc.vector.tensor_copy(ident_bf[:], ident)
                nc.vector.tensor_copy(causal_bf[:], w("causal"))
                dve.wait_ge(composed, 2)
                nc.vector.tensor_copy(F1[:], PS[0][:, 0])
                nc.vector.tensor_copy(F2[:], PS[0][:, 1].rearrange("p (f n) -> p f n", f=4))
                dve.drain()

            @block.tensor
            def _(pe):
                pe.wait_ge(scaled, 1)
                pe.wait_ge(fc_in[1], 32)
                for c in range(16):
                    mm = nc.tensor.matmul(PS[0][:, 0], A1[:, c], B1[:, c], start=(c == 0), stop=(c == 15))
                mm.then_inc(composed, 1)
                pe.wait_ge(scaled, 2)
                pe.wait_ge(fc_in[3], 32)
                for f in range(4):
                    for c in range(16):
                        mm = nc.tensor.matmul(PS[0][:, 1, 128 * f:128 * f + 128],
                                              A2[:, c, 128 * f:128 * f + 128], B2[:, c],
                                              start=(c == 0), stop=(c == 15))
                mm.then_inc(composed, 1)

        nc.clear_and_free_semaphores(pre_sems)
        nc.all_engine_barrier()

        xTs = lane("x_T", [128, 128])
        cs = lane("ctx_rows", [128, D])
        cTs = lane("ctx_T", [128, 128])
        ms = lane("mask_i", [128, 128], I32)
        madd = lane("mask_add", [128, 128], BF16)
        q4 = lane("q4", [128, TG, 128])
        k4 = lane("k4", [128, TJ, 128])
        q1 = lane("q1", [128, 128])
        k1 = lane("k1", [128, M + 128])
        ql = lane("q_landmark", [128, M])
        qlm = lane("q_landmarks", [128, H, M])
        klm = lane("k_landmarks", [128, H, M])
        e1 = lane("e1", [128, H, M])
        p2 = lane("p2", [128, PAIRS, M])
        e3 = lane("e3", [128, PAIRS, 128])
        e1T = lane("e1T", [128, PAIRS, 128])
        e3T = lane("e3T", [128, PAIRS, 128])
        k2T = lane("k2T", [128, 4, 128])
        ss = lane("ss", [128, PAIRS, PW])
        wz = lane("wz", [128, PAIRS, PW])
        uu = lane("uu", [128, PAIRS, HD])
        pe_ = [[sb(f"probs{s}{g}", [128, 4, 128]) for g in range(2)] for s in lanes]
        pT = [[sb(f"probsT{s}{g}", [128, 4, 128]) for g in range(2)] for s in lanes]
        small = lane("small", [128, 192])
        oT = lane("oT", [128, TG, 128])
        z = lane("z", [128, H, HD])
        zT = lane("zT", [128, 128])
        res = lane("res", [128, D])
        xbo = lane("x_plus_bo", [128, D])
        cn = lane("ctx_norm", [128, D])
        xn = lane("x_norm", [128, D])
        cnT = lane("ctx_normT", [128, 128])
        xnT = lane("x_normT", [128, 128])
        q8, k8, o8 = e1T, e3, e3T
        v8 = lane("v8", [128, 2, 512])
        hT = [[e1[s][:, 8 * g:8 * g + 8].rearrange("p (a x) b -> p a (x b)", x=2) for g in range(2)] for s in lanes]
        gT = lane("gateT", [EXPERTS, 128])

        made, names = {}, {}

        def sem(name, s=None):
            key = name if s is None else f"{name}{s}"
            if key not in made:
                names[key] = names.get(key, 0) + 1
                made[key] = nc.alloc_semaphore(f"{key}_{names[key]}")
            return made[key]

        def one_block(streams, first, last):
            with nc.Block() as block:
                body(nc, block, streams, first, last, sem, everything)
            nc.clear_and_free_semaphores([made.pop(key) for key in list(made) if streams == "r" or key.startswith("n_")])
            nc.all_engine_barrier()

        everything = dict(locals())
        with nc.Fori(0, B // LANES - 1) as turn:
            one_block("n", turn * LANES, False)
            one_block("r", turn * LANES, False)
        one_block("n", B - LANES, True)
        one_block("r", B - LANES, True)
        with nc.Block() as block:
            @block.sync
            def _(sp):
                for s in lanes:
                    sp.wait_ge(stored[s], 16 * (B // LANES) + 16)


def body(nc, block, kind, first, last, sem, o):
    (x, xT, ctx, ctxT, mask, out, W, R, b2s, F1, F2, kaug, ident_bf, causal_bf, w, row, ident) = (
        o[k] for k in "x xT ctx ctxT mask out W R b2s F1 F2 kaug ident_bf causal_bf w row ident".split())
    (stored, xin, xTin, xs, xTs, cs, cTs, ms, madd, q4, k4, q1, k1, ql, qlm, klm, v9, w9, e1, p2, e3, e1T, e3T, k2T, ey, ss, wz, uu, pe_, pT) = (
        o[k] for k in "stored xin xTin xs xTs cs cTs ms madd q4 k4 q1 k1 ql qlm klm v9 w9 e1 p2 e3 e1T e3T k2T ey ss wz uu pe_ pT".split())
    (oT, z, zT, res, xbo, cn, xn, cnT, xnT, q8, k8, v8, o8, hT, gT, PS, sm, over, every) = (
        o[k] for k in "oT z zT res xbo cn xn cnT xnT q8 k8 v8 o8 hT gT PS sm over every".split())

    def bank(s, b, a=0, n=512):
        return PS[s][:, b, a:a + n]

    def heads(h):
        g, j = divmod(h, TJ)
        p, m = divmod(h, 2)
        return g, slice(TW * j, TW * j + TW), p, slice(M * m, M * m + M)

    def k_alone(s, g):
        return (ss, wz)[g // 2][s][:, 4 * (g % 2):4 * (g % 2) + 4, 0:2 * M]

    halves = [slice(M * m, M * m + M) for m in range(2)]

    def product(k, step, g):
        a, b = GROUPS[g]
        return (2 * len(GROUPS) * k + len(GROUPS) * step + g) % 4, range(a, b)

    def pairs_of(s, k, step, g):
        bk, ps = product(k, step, g)
        return bank(s, bk, 0, PW * len(ps)).rearrange("p (a b) -> p a b", b=PW), slice(ps[0], ps[-1] + 1)

    lanes = range(LANES)
    plan = [(s, name) for _, s, name in sorted(
        (place + s * LAG[kind], s, name) for s in lanes for place, name in (N_SLOTS if kind == "n" else R_SLOTS))]

    def run(nystrom, rest):
        streams = [(nystrom if kind == "n" else rest)(s) for s in lanes]
        for s, name in plan:
            assert next(streams[s]) == name, name

    @block.sync
    def _(sp):
        if kind == "n":
            for s in lanes:
                sp.dma_start(cTs[s][:], ctxT[first + s]).then_inc(sem("ctx_in", s), 16)
                sp.dma_start(cs[s][:], ctx[first + s]).then_inc(sem("ctx_in", s), 16)
                sp.dma_start(ms[s][:], mask[first + s]).then_inc(sem("ctx_in", s), 16)
            return
        if not last:
            for s in lanes:
                sp.dma_start(xin[s][:], x[first + (LANES + s)]).then_inc(sem("x_in", s), 16)
                sp.dma_start(xTin[s][:], xT[first + (LANES + s)]).then_inc(sem("x_in", s), 16)
            for s in lanes:
                sp.wait_ge(sem("x_in", s), 32)
        for s in lanes:
            sp.wait_ge(sem("ln_rows", s), 6)
            sp.dma_start(out[first + s], xs[s][:]).then_inc(stored[s], 16)

    @block.tensor
    def _(pe):
        mmul = nc.tensor.matmul

        def one(dst, lhsT, rhs):
            return mmul(dst, lhsT, rhs, start=True, stop=True)

        def turned(dst, src):
            return nc.tensor.transpose(dst, src, ident)

        def project(s, wq, wk, wv, src, sig, q_src=None):
            for b, (name, t) in enumerate(((wq, q_src or xTs[s]), (wk, src))):
                for g in range(WCOL[name][1] // 128):
                    mm = one(bank(s, b, 128 * g, 128), w(name, 128 * g, 128), t[:])
                mm.then_inc(sem(sig, s), 1)
            one(bank(s, 2, 0, D), src[:], w(wv)).then_inc(sem(sig, s), 1)

        def tail_turn(s, n):
            pe.wait_ge(sem("oT", s), n)
            for g in range(TG):
                mm = turned(bank(s, 0, 128 * g, 128), oT[s][:, g])
            mm.then_inc(sem("o_rows", s), 1)

        def tail_zT(s, n):
            pe.wait_ge(sem("z", s), n)
            turned(bank(s, 2, 0, 128), z[s][:].rearrange("p h e -> p (h e)")).then_inc(sem("zT_ps", s), 1)

        def tail_out(s, n, wp):
            pe.wait_ge(sem("zT", s), n)
            one(bank(s, 2, 128, D), zT[s][:], w(wp)).then_inc(sem("sub", s), 1)

        def ln_turn(s, n):
            pe.wait_ge(sem("ln_rows", s), n)
            turned(bank(s, 0, 0, 128), xs[s][:]).then_inc(sem("ln_T_ps", s), 1)

        def nystrom(s):
            project(s, "n_q", "n_k", "n_v", xTin[s], "n_proj", xTin[s])
            yield "n.proj"
            for half in range(2):
                tiles = (2 * half, 2 * half + 1)
                if half == 0:
                    pe.wait_ge(sem("n_lm", s), 2)
                else:
                    pe.wait_ge(sem("n_lm_pool", s), 2)
                    pe.wait_ge(sem("n_e1", s), 1)
                for g in tiles:
                    one(bank(s, g % 2, 0, TJ * M), q1[s][:], klm[s][:, TJ * g:TJ * g + TJ].rearrange("p a b -> p (a b)")
                        ).then_inc(sem("n_k1", s), 1)
                if half == 0:
                    pe.wait_ge(sem("n_v9", s), 1)
                else:
                    pe.wait_ge(sem("n_e23", s), 1)
                for c in range(2):
                    for g in tiles:
                        mm = one(bank(s, 2 + g % 2, 192 * c, 192),
                                 qlm[s][:, TJ * g + 2 * c:TJ * g + 2 * c + 2].rearrange("p a b -> p (a b)"), k1[s][:])
                        if c == 1:
                            mm.then_inc(sem("n_k23", s), 1)
                yield f"n.s{half}"
            pe.wait_ge(sem("n_e1", s), 2)
            for half in range(2):
                pe.wait_ge(sem("n_p2", s), half + 1)
                one(bank(s, 0, 256 * half, 256), w("ones2"),
                    p2[s][:, 4 * half:4 * half + 4].rearrange("p a b -> p (a b)")).then_inc(sem("n_colsum", s), 1)
                for i in (2 * half, 2 * half + 1):
                    mm = turned(bank(s, 1, 128 * i, 128), p2[s][:, 2 * i:2 * i + 2].rearrange("p a b -> p (a b)"))
                mm.then_inc(sem("n_k2T_ps", s), 1)
                yield f"n.col{half}"
            pe.wait_ge(sem("n_e23", s), 2)
            for p in range(PAIRS):
                mm = turned(bank(s, 2 + p // 4, 128 * (p % 4), 128), e3[s][:, p])
                if p % 4 == 3:
                    mm.then_inc(sem("n_e3T_ps", s), 1)
            yield "n.e3T"
            for p in range(PAIRS):
                if p % 4 == 0:
                    pe.wait_ge(sem("n_e3T", s), p // 4 + 1)
                mm = turned(bank(s, 2 + p // 4, 128 * (p % 4), 128),
                            e1[s][:, 2 * p:2 * p + 2].rearrange("p a b -> p (a b)"))
                if p % 4 == 3:
                    mm.then_inc(sem("n_e1T_ps", s), 1)
            yield "n.e1T"
            pe.wait_ge(sem("n_rd", s), 1)
            pe.wait_ge(sem("n_k2T", s), 1)
            for c in range(2):
                for i in range(4):
                    for m in halves:
                        t = k2T[s][M * c:M * c + M, i, m]
                        mm = one(PS[s][m, c, M * i:M * i + M], t, t)
                mm.then_inc(sem("n_kkT", s), 1)
            yield "n.kkT"
            pe.wait_ge(sem("n_e1T", s), 2)
            for h in range(H):
                _, _, p, m = heads(h)
                mm = one(PS[s][m, 2, 16 * p:16 * p + HD + 1], e3T[s][:, p, m], v9[s][:, h, 0:HD + 1])
            mm.then_inc(sem("n_y0", s), 1)
            yield "n.y0"
            pe.wait_ge(sem("n_E0", s), 1)
            pe.wait_ge(sem("n_y", s), 1)
            for k in range(NEWTON):
                for g in range(3):
                    if k:
                        pe.wait_ge(sem("n_e", s), 3 * (k - 1) + g + 1)
                        pe.wait_ge(sem("n_y", s), 3 * (k - 1) + g + 2)
                    bk, ps = product(k, 0, g)
                    for i, p in enumerate(ps):
                        mm = one(bank(s, bk, PW * i, PW), ey[s][:, p, 0:2 * M], ey[s][:, p])
                    mm.then_inc(sem("n_S_ps", s), 1)
                    yield f"n.S{k}{g}"
                for g in range(3):
                    pe.wait_ge(sem("n_wz", s), 3 * k + g + 1)
                    a = 0 if k < NEWTON - 1 else 2 * M
                    bk, ps = product(k, 1, g)
                    for i, p in enumerate(ps):
                        mm = one(bank(s, bk, PW * i + a, PW - a), ss[s][:, p, 0:2 * M], wz[s][:, p, a:PW])
                    mm.then_inc(sem("n_SW", s), 1)
                    yield f"n.W{k}{g}"
            pe.wait_ge(sem("n_y", s), 3 * NEWTON + 1)
            for h in range(H):
                _, _, p, m = heads(h)
                mm = one(PS[s][m, 0, 16 * p:16 * p + HD], p2[s][m, p], ey[s][m, p, 2 * M:PW])
            mm.then_inc(sem("n_w_ps", s), 1)
            yield "n.w"
            pe.wait_ge(sem("n_w9", s), 1)
            for h in range(H):
                g, r, p, m = heads(h)
                mm = one(PS[s][r, 3, 128 * g:128 * g + 128], w9[s][m, p], e1T[s][m, p])
            mm.then_inc(sem("o_ps", s), 1)
            yield "n.o"
            tail_turn(s, 1)
            yield "n.rows"
            tail_zT(s, 1)
            yield "n.z"
            tail_out(s, 1, "n_p")
            yield "n.out"
            ln_turn(s, 1)
            yield "n.ln"

        def beside(s, n_att, half):
            b = 1 + 2 * half
            if n_att == 1:
                pe.wait_ge(sem("y_T", s), 1)
                for c in range(4):
                    mm = one(bank(s, b, 128 * c, 128), w("y_k", 512 * half + 128 * c, 128), cnT[s][:])
                mm.then_inc(sem("y_qk_ps", s), 1)
            else:
                one(bank(s, b), cnT[s][:], w("y_v", 512 * half, 512)).then_inc(sem("y_v_ps", s), 1)

        def attention8(s, names, srcs, n_ln, n_att, masked):
            pe.wait_ge(sem("xT", s), n_ln)
            if srcs is cTs:
                pe.wait_ge(sem("ctx_in", s), 48)
            project(s, *names[:3], srcs[s], "a_proj")
            yield f"r{n_att}.proj"

            def scores(s, pair):
                if pair == 0:
                    pe.wait_ge(sem("a_q", s), n_att)
                    pe.wait_ge(sem("a_k01", s), 2 * n_att)
                else:
                    pe.wait_ge(sem("a_k23", s), 2 * n_att)
                    pe.wait_ge(sem("a_p", s), 4 * (n_att - 1) + 2)
                groups = (2 * pair, 2 * pair + 1)
                if masked:
                    for g in groups:
                        mmul(bank(s, g % 2).rearrange("p (a b) -> p a b", a=4), ident_bf[:],
                             every(causal_bf[:], 4), start=True, stop=False, skip_group_check=True)
                    for g in groups:
                        mmul(bank(s, g % 2).rearrange("p (a b) -> p a b", a=4), q1[s][:], k_alone(s, g),
                             start=False, stop=True, skip_group_check=True).then_inc(sem("a_s", s), 1)
                    return
                for j in range(TJ):
                    for g in groups:
                        mm = one(bank(s, g % 2, 128 * j, 128), q4[s][:, j], k_alone(s, g)[:, j])
                        if j == TJ - 1:
                            mm.then_inc(sem("a_s", s), 1)

            def turn_probs(s, g):
                pe.wait_ge(sem("a_p", s), 4 * (n_att - 1) + g + 1)
                if g == 0:
                    pe.wait_ge(sem("a_v9", s), n_att)
                else:
                    pe.wait_ge(sem("a_pT", s), 4 * (n_att - 1) + g)
                for j in range(TJ):
                    mm = turned(bank(s, 2, 128 * j, 128), pe_[s][g % 2][:, j])
                mm.then_inc(sem("a_pT_ps", s), 1)

            def values(s, g):
                pe.wait_ge(sem("a_pT", s), 4 * (n_att - 1) + g + 1)
                for i in range(TG):
                    mm = one(PS[s][TW * i:TW * i + TW, 3, 128 * g:128 * g + 128], v9[s][:, TJ * g + i], pT[s][g % 2][:, i])
                mm.then_inc(sem("a_pv", s), 1)

            scores(s, 0)
            yield f"r{n_att}.first"
            for g in range(TG):
                if g:
                    values(s, g - 1)
                yield f"r{n_att}.s{g}"
                turn_probs(s, g)
                if g == 1:
                    scores(s, 1)
                yield f"r{n_att}.t{g}"
            values(s, 3)
            yield f"r{n_att}.last"
            tail_turn(s, 1 + n_att)
            if n_att == 1:
                pe.wait_ge(sem("y_cn", s), 1)
                turned(bank(s, 1, 0, 128), cn[s][:]).then_inc(sem("y_cnT_ps", s), 1)
            yield f"r{n_att}.rows"
            tail_zT(s, 1 + n_att)
            beside(s, n_att, 0)
            yield f"r{n_att}.z"
            tail_out(s, 1 + n_att, names[3])
            beside(s, n_att, 1)
            yield f"r{n_att}.out"

        def rest(s):
            yield from attention8(s, ("x_q4", "x_k4", "x_v", "x_p"), cTs, 1, 1, False)
            ln_turn(s, 2)
            yield "r.ln2"

            pe.wait_ge(sem("xT", s), 2)
            pe.wait_ge(sem("y_qk", s), 2)
            one(bank(s, 3, 0, EXPERTS), xTs[s][:], w("m_r")).then_inc(sem("m_logits", s), 1)

            def hidden(s, t):
                if t >= 2:
                    pe.wait_ge(sem(f"m_h{t % 2}", s), 1)
                for c in range(4):
                    mm = one(bank(s, t % 2, 128 * c, 128), w("m_1", 512 * t + 128 * c, 128), xTs[s][:])
                mm.then_inc(sem("m_h_ps", s), 1)

            hidden(s, 0)
            yield "rm.first"
            for t in range(4):
                if t < 3:
                    hidden(s, t + 1)
                yield f"rm.h{t}"
                pe.wait_ge(sem(f"m_h{t % 2}", s), t // 2 + 1)
                if t == 1:
                    pe.wait_ge(sem("m_res", s), 1)
                if t >= 2:
                    pe.wait_ge(sem("m_y_used", s), 2 * (t - 1))
                for e in (2 * t, 2 * t + 1):
                    for c in range(2):
                        mm = mmul(bank(s, 2 + t % 2, 128 * (e % 2), 128), hT[s][t % 2][:, 2 * (e % 2) + c],
                                  w("m_2", (2 * e + c) * 128, 128), start=(c == 0), stop=(c == 1))
                mm.then_inc(sem("m_y", s), 1)
                if t == 0:
                    pe.wait_ge(sem("m_gate", s), 1)
                    turned(PS[s][0:EXPERTS, 3, 128:256], sm(s, "gate")).then_inc(sem("m_gT_ps", s), 1)
                    pe.wait_ge(sem("m_gT", s), 1)
                    one(bank(s, 3, 256, D), gT[s][:], b2s[:]).then_inc(sem("m_b2", s), 1)
                yield f"rm.y{t}"
            ln_turn(s, 3)
            yield "r.ln3"

            yield from attention8(s, ("c_q", "c_k", "c_v", "c_p"), xTs, 3, 2, True)
            ln_turn(s, 4)
            yield "r.ln4"

            yield "ry.stats"
            pe.wait_ge(sem("y_v8", s), 1)
            pe.wait_ge(sem("y_xn", s), 1)
            turned(bank(s, 1, 128, 128), xn[s][:]).then_inc(sem("y_xnT_ps", s), 1)
            yield "ry.norm"
            yield "ry.T"
            pe.wait_ge(sem("y_T", s), 2)
            pe.wait_ge(sem("xT", s), 4)
            for b in range(2):
                for c in range(4):
                    mm = one(bank(s, b, 128 * c, 128), w("y_q", 512 * b + 128 * c, 128), xnT[s][:])
                mm.then_inc(sem("y_qk_ps", s), 1)
                yield f"ry.q{b}"

            def yscores(s, pair):
                if pair == 0:
                    pe.wait_ge(sem("y_qk", s), 4)
                    pe.wait_ge(sem("y_mask", s), 1)
                    pe.wait_ge(sem("y_v8", s), 2)
                else:
                    pe.wait_ge(sem("y_e", s), 2)
                groups = (2 * pair, 2 * pair + 1)
                for g in groups:
                    mmul(bank(s, g % 2).rearrange("p (a b) -> p a b", a=4), ident_bf[:],
                         every(madd[s][:], 4), start=True, stop=False, skip_group_check=True)
                for j in range(4):
                    for g in groups:
                        h = y_head(g, j)
                        r = slice(64 * (h % 2), 64 * (h % 2) + 64)
                        mm = mmul(bank(s, g % 2, 128 * j, 128), q8[s][r, h // 2], k8[s][r, h // 2],
                                  start=False, stop=True, skip_group_check=True)
                        if j == 3:
                            mm.then_inc(sem("y_s", s), 1)

            def y_values(s, g):
                pe.wait_ge(sem("y_pT", s), g + 1)
                if g:
                    pe.wait_ge(sem("y_o8", s), g)
                for j in range(4):
                    h = y_head(g, j)
                    c = 256 * (g % 2) + 64 * j
                    for m in range(2):
                        mm = one(PS[s][64 * m:64 * m + 64, 3, c:c + 64],
                                 v8[s][:, h // 8, 64 * (h % 8):64 * (h % 8) + 64], pT[s][g % 2][:, j, m::2])
                mm.then_inc(sem("y_pv", s), 1)

            yscores(s, 0)
            yield "ry.first"
            for g in range(4):
                if g:
                    y_values(s, g - 1)
                yield f"ry.s{g}"
                pe.wait_ge(sem("y_p", s), 2 * g + 2)
                if g:
                    pe.wait_ge(sem("y_pT", s), g)
                for j in range(4):
                    mm = turned(bank(s, 2, 128 * j, 128), pe_[s][g % 2][:, j])
                mm.then_inc(sem("y_pT_ps", s), 1)
                if g == 1:
                    yscores(s, 1)
                yield f"ry.t{g}"
            y_values(s, 3)
            yield "ry.last"
            pe.wait_ge(sem("y_o8", s), 4)
            for t in range(8):
                mm = mmul(bank(s, 2, 128, D), o8[s][:].rearrange("p a b -> p (a b)")[:, t::8], w("y_p", 128 * t, 128),
                          start=(t == 0), stop=(t == 7))
            mm.then_inc(sem("sub", s), 1)
            yield "ry.out"
            ln_turn(s, 5)
            yield "r.ln5"

            pe.wait_ge(sem("xT", s), 5)
            for c in range(4):
                mm = one(bank(s, 1, 128 * c, 128), F1[:, 128 * c:128 * c + 128], xTs[s][:])
            mm.then_inc(sem("f_h_ps", s), 1)
            yield "rf.h"
            yield "rf.u"
            pe.wait_ge(sem("f_g", s), 1)
            for c in range(4):
                mm = mmul(bank(s, 2, 128, D), hT[s][1][:, c], F2[:, c], start=(c == 0), stop=(c == 3))
            mm.then_inc(sem("sub", s), 1)
            yield "rf.out"
            yield "rf.ln"

        run(nystrom, rest)

    @block.scalar
    def _(act):
        copy = nc.scalar.copy

        def tail(s, n):
            copy(oT[s][:].rearrange("p g q -> p (g q)"), bank(s, 3)).then_inc(sem("oT", s), 1)

        def tail_zT(s, n):
            act.wait_ge(sem("zT_ps", s), n)
            copy(zT[s][:], bank(s, 2, 0, 128)).then_inc(sem("zT", s), 1)

        def ln_T(s, n):
            act.wait_ge(sem("ln_T_ps", s), n)
            copy(xTs[s][:], bank(s, 0, 0, 128)).then_inc(sem("xT", s), 1)

        def nystrom(s):
            act.wait_ge(sem("n_proj", s), 1)
            copy(q1[s][:], bank(s, 0, 0, 128)).then_inc(sem("n_qk", s), 1)
            act.wait_ge(sem("n_proj", s), 2)
            copy(k1[s][:, M:M + 128], bank(s, 1, 0, 128)).then_inc(sem("n_qk", s), 1)
            yield "n.proj"
            for half in range(2):
                act.wait_ge(sem("n_nb1", s), half + 1)
                for h in range(8 * half, 8 * half + 8):
                    ins = nc.scalar.activation(e1[s][:, h], bank(s, h // TJ % 2, M * (h % TJ), M), ACT.Exp,
                                               bias=sm(s, "nb1", h, 1), scale=0.5 * SC8)
                ins.then_inc(sem("n_e1", s), 1)
                act.wait_ge(sem("n_s23", s), half + 1)
                v = p2[s][:, 4 * half:4 * half + 4]
                nc.scalar.activation(v, v, ACT.Exp, scale=0.25 * SC8).then_inc(sem("n_e2", s), 1)
                for p in range(4 * half, 4 * half + 4):
                    ins = nc.scalar.activation(e3[s][:, p], bank(s, 2 + p // 2 % 2, 192 * (p % 2) + M, 128), ACT.Exp,
                                               bias=sm(s, "nb3", p, 1), scale=0.5 * SC8)
                ins.then_inc(sem("n_e23", s), 1)
                yield f"n.s{half}"
            yield "n.col0"
            act.wait_ge(sem("n_k2T_ps", s), 2)
            copy(k2T[s][:].rearrange("p a b -> p (a b)"), bank(s, 1)).then_inc(sem("n_k2T", s), 1)
            yield "n.col1"
            for half in range(2):
                act.wait_ge(sem("n_e3T_ps", s), half + 1)
                copy(e3T[s][:, 4 * half:4 * half + 4].rearrange("p a b -> p (a b)"), bank(s, 2 + half)).then_inc(sem("n_e3T", s), 1)
            yield "n.e3T"
            for half in range(2):
                act.wait_ge(sem("n_e1T_ps", s), half + 1)
                copy(e1T[s][:, 4 * half:4 * half + 4].rearrange("p a b -> p (a b)"), bank(s, 2 + half)).then_inc(sem("n_e1T", s), 1)
            yield "n.e1T"
            yield "n.kkT"
            yield "n.y0"
            for k in range(NEWTON):
                for g in range(3):
                    act.wait_ge(sem("n_S_ps", s), 3 * k + g + 1)
                    src, ps = pairs_of(s, k, 0, g)
                    copy(ss[s][:, ps], src).then_inc(sem("n_S", s), 1)
                    yield f"n.S{k}{g}"
                for g in range(3):
                    if k < NEWTON - 1:
                        act.wait_ge(sem("n_SW", s), 3 * k + g + 1)
                        src, ps = pairs_of(s, k, 1, g)
                        nc.scalar.mul(ey[s][:, ps], src, 0.25).then_inc(sem("n_e", s), 1)
                    yield f"n.W{k}{g}"
            yield "n.w"
            act.wait_ge(sem("o_ps", s), 1)
            tail(s, 1)
            yield "n.o"
            yield "n.rows"
            tail_zT(s, 1)
            yield "n.z"
            yield "n.out"
            ln_T(s, 1)
            yield "n.ln"

        def attention8(s, n_att, plain, n_ln):
            if plain:
                act.wait_ge(sem("a_proj", s), 3 * (n_att - 1) + 1)
                copy(q1[s][:], bank(s, 0, 0, 128)).then_inc(sem("a_q", s), 1)
            yield f"r{n_att}.proj"
            yield f"r{n_att}.first"
            for g in range(TG):
                n = 4 * (n_att - 1) + g
                act.wait_ge(sem("a_nb", s), n + 1)
                if g >= 2:
                    act.wait_ge(sem("a_pT_ps", s), n - 1)
                for j in range(TJ):
                    ins = nc.scalar.activation(pe_[s][g % 2][:, j], bank(s, g % 2, 128 * j, 128), ACT.Exp,
                                               bias=sm(s, "nb", 4 * g + j, 1), scale=SC8)
                ins.then_inc(sem("a_p", s), 1)
                yield f"r{n_att}.s{g}"
                yield f"r{n_att}.t{g}"
            act.wait_ge(sem("a_pv", s), 4 * n_att)
            tail(s, 1 + n_att)
            yield f"r{n_att}.last"
            yield f"r{n_att}.rows"
            tail_zT(s, 1 + n_att)
            yield f"r{n_att}.z"
            yield f"r{n_att}.out"
            ln_T(s, n_ln)
            yield f"r.ln{n_ln}"

        def rest(s):
            yield from attention8(s, 1, False, 2)
            act.wait_ge(sem("m_pnb", s), 1)
            nc.scalar.activation(sm(s, "e8"), sm(s, "lg"), ACT.Exp, bias=sm(s, "pnb"),
                                 accum_out=sm(s, "psum")).then_inc(sem("m_e8", s), 1)
            yield "rm.first"
            for t in range(4):
                if t % 2 == 0:
                    act.wait_ge(sem("m_h_ps", s), t + 1)
                    if t >= 2:
                        act.wait_ge(sem("m_y", s), t - 1)
                    for c in range(4):
                        ins = nc.scalar.activation(hT[s][t % 2][:, c], bank(s, t % 2, 128 * c, 128), ACT.Relu,
                                                   bias=w("m_b1", 4 * t + c, 1))
                    ins.then_inc(sem("m_h0", s), 1)
                yield f"rm.h{t}"
                if t == 0:
                    act.wait_ge(sem("m_gT_ps", s), 1)
                    copy(gT[s][:], PS[s][0:EXPERTS, 3, 128:256]).then_inc(sem("m_gT", s), 1)
                yield f"rm.y{t}"
            ln_T(s, 3)
            yield "r.ln3"
            yield from attention8(s, 2, True, 4)
            for name in ("stats", "norm", "T"):
                yield f"ry.{name}"
            for b in range(2):
                yield f"ry.q{b}"
            yield "ry.first"
            for g in range(4):
                act.wait_ge(sem("y_nb", s), g + 1)
                if g >= 2:
                    act.wait_ge(sem("y_pT_ps", s), g - 1)
                for j in range(4):
                    ins = nc.scalar.activation(pe_[s][g % 2][:, j], bank(s, g % 2, 128 * j, 128), ACT.Exp,
                                               bias=sm(s, "nb", 4 * g + j, 1), scale=SC64,
                                               accum_out=sm(s, "rs", 4 * g + j, 1))
                ins.then_inc(sem("y_e", s), 1)
                if g:
                    y_o8(nc, act, sem, s, g - 1, o8, PS)
                yield f"ry.s{g}"
                yield f"ry.t{g}"
            y_o8(nc, act, sem, s, 3, o8, PS)
            yield "ry.last"
            yield "ry.out"
            ln_T(s, 5)
            yield "r.ln5"
            act.wait_ge(sem("f_h_ps", s), 1)
            nc.scalar.activation(hT[s][1][:].rearrange("p a b -> p (a b)"), bank(s, 1), ACT.Square, scale=GELU_A ** 0.5)
            copy(hT[s][0][:].rearrange("p a b -> p (a b)"), bank(s, 1)).then_inc(sem("f_h", s), 1)
            yield "rf.h"
            act.wait_ge(sem("f_u", s), 1)
            nc.scalar.activation(hT[s][1][:], hT[s][1][:], ACT.Tanh, scale=GELU_C).then_inc(sem("f_t", s), 1)
            yield "rf.u"
            yield "rf.out"
            yield "rf.ln"

        run(nystrom, rest)

    @block.gpsimd
    def _(pool):
        def slots(s, work, all_slots):
            for _, name in all_slots:
                if name in work:
                    work[name](s)
                yield name

        def rstd(s, n, ve="ve", out="rstd", ready="ln_ve", done="ln_rstd"):
            pool.wait_ge(sem(ready, s), n)
            nc.gpsimd.tensor_tensor(sm(s, out), sm(s, ve), w("mhalf"), ALU.pow).then_inc(sem(done, s), 1)

        def xbo_after(s, n, bias):
            pool.wait_ge(sem("ln_rows", s), n)
            nc.gpsimd.tensor_tensor(xbo[s][:], xs[s][:], row(bias), ALU.add).then_inc(sem("xbo", s), 1)

        def alone(s, n):
            pool.wait_ge(sem("a_k4", s), n)
            for g in (2, 3):
                nc.gpsimd.tensor_scalar(k_alone(s, g), k4[s][:], w("gmask", g, 1), None, ALU.mult).then_inc(sem("a_k23", s), 1)

        def y_scale(g):
            def scale(s):
                pool.wait_ge(sem("y_rs", s), g + 1)
                v = pe_[s][g % 2][:, 0:2]
                nc.gpsimd.tensor_tensor(v, v, over(sm(s, "rs", 4 * g, 2), 128), ALU.mult).then_inc(sem("y_p", s), 1)
            return scale

        def landmarks(s):
            for t, (src, dst) in enumerate(((ql[s][:], qlm[s][:]), (k1[s][:, 0:M], klm[s][:]))):
                pool.wait_ge(sem("n_sum", s), t + 1)
                nc.gpsimd.tensor_tensor(dst[:, H // 2:H], every(src, H // 2), over(w("mask16", H // 2, H // 2), M), ALU.mult
                                        ).then_inc(sem("n_lm_pool", s), 1)

        def nystrom(s):
            return slots(s, {"n.proj": landmarks, "n.out": lambda s: rstd(s, 1)}, N_SLOTS)

        def rest(s):
            work = {"r1.proj": lambda s: alone(s, 1), "r2.proj": lambda s: alone(s, 2),
                    "r.ln3": lambda s: xbo_after(s, 3, "c_bo"), "ry.stats": lambda s: (rstd(s, 5), xbo_after(s, 4, "y_bo")),
                    "r1.t3": lambda s: rstd(s, 1, "cve", "crstd", "y_cve", "y_crstd"),
                    "r1.out": lambda s: rstd(s, 2), "rm.y3": lambda s: rstd(s, 3), "r2.out": lambda s: rstd(s, 4),
                    "ry.out": lambda s: rstd(s, 6), "rf.out": lambda s: rstd(s, 7)}
            for g in range(4):
                work[f"ry.s{g}"] = y_scale(g)
            return slots(s, work, R_SLOTS)

        run(nystrom, rest)

    @block.vector
    def _(dve):
        V = nc.vector
        count = [0]

        def link(ins):
            count[0] += 1
            ins.then_inc(sem(f"{kind}_vector_steps"), 1)
            dve.wait_ge(sem(f"{kind}_vector_steps"), count[0])

        def stats(s, src, st, mv, ve):
            link(V.bn_stats(sm(s, st), src))
            link(V.bn_aggr(sm(s, mv), sm(s, st)))
            return V.tensor_scalar(sm(s, ve), sm(s, mv, 1, 1), EPS, None, ALU.add)

        def ln_stats(s, n, residual):
            dve.wait_ge(sem("sub", s), n)
            link(V.tensor_tensor(res[s][:], bank(s, 2, 128, D), residual, ALU.add))

        def ln_rows(s, n, n_rstd):
            dve.wait_ge(sem("ln_rstd", s), n_rstd)
            V.tensor_scalar(xs[s][:], res[s][:], sm(s, "mv", 0, 1), sm(s, "rstd"),
                            ALU.subtract, ALU.mult).then_inc(sem("ln_rows", s), 1)

        def tail(s, n):
            dve.wait_ge(sem("o_rows", s), n)
            v = bank(s, 0).rearrange("p (h e) -> p h e", e=TW)
            link(V.reciprocal(sm(s, "rs"), v[:, :, HD]))
            V.tensor_tensor(z[s][:], v[:, :, 0:HD], over(sm(s, "rs"), HD), ALU.mult).then_inc(sem("z", s), 1)

        def nystrom(s):
            for t, (src, dst, alone) in enumerate(((q1[s][:], ql[s][:], qlm[s][:]),
                                                   (k1[s][:, M:M + 128], k1[s][:, 0:M], klm[s][:]))):
                dve.wait_ge(sem("n_qk", s), t + 1)
                V.tensor_tensor(dst, src[:, 0:128:2], src[:, 1:128:2], ALU.add).then_inc(sem("n_sum", s), 1)
                dve.wait_ge(sem("n_sum", s), t + 1)
                V.tensor_tensor(alone[:, 0:H // 2], every(dst, H // 2), over(w("mask16", 0, H // 2), M), ALU.mult
                                ).then_inc(sem("n_lm", s), 1)
            dve.wait_ge(sem("n_proj", s), 3)
            V.tensor_copy(v9[s][:, :, 0:HD], bank(s, 2, 0, D).rearrange("p (h e) -> p h e", e=HD)).then_inc(sem("n_v9", s), 1)

            yield "n.proj"

            def kernel1(s, half):
                for g in (2 * half, 2 * half + 1):
                    dve.wait_ge(sem("n_k1", s), g + 1)
                    ins = V.tensor_reduce(sm(s, "mx1", TJ * g, TJ), bank(s, g % 2, 0, 256).rearrange("p (h m) -> p h m", m=M),
                                          AX, ALU.max)
                link(ins)
                V.tensor_scalar(sm(s, "nb1", 8 * half, 8), sm(s, "mx1", 8 * half, 8), -0.5 * SC8, None, ALU.mult
                                ).then_inc(sem("n_nb1", s), 1)

            def kernels23(s, half):
                tiles = (2 * half, 2 * half + 1)
                v = [bank(s, 2 + t % 2, 0, 384).rearrange("p (a b) -> p a b", a=2) for t in tiles]
                for i, t in enumerate(tiles):
                    dve.wait_ge(sem("n_k23", s), t + 1)
                    V.tensor_reduce(sm(s, "mx2", 2 * t, 2), v[i][:, :, 0:M], AX, ALU.max)
                    ins = V.tensor_reduce(sm(s, "mx3", 2 * t, 2), v[i][:, :, M:192], AX, ALU.max)
                link(ins)
                for i, t in enumerate(tiles):
                    V.tensor_tensor(p2[s][:, 2 * t:2 * t + 2], v[i][:, :, 0:M], over(sm(s, "mx2", 2 * t, 2), M), ALU.subtract)
                V.tensor_scalar(sm(s, "nb3", 4 * half, 4), sm(s, "mx3", 4 * half, 4), -0.5 * SC8, None, ALU.mult
                                ).then_inc(sem("n_s23", s), 1)

            def normalise(s, half):
                dve.wait_ge(sem("n_e2", s), half + 1)
                v = p2[s][:, 4 * half:4 * half + 4]
                r = sm(s, "rs2", 4 * half, 4)
                link(V.tensor_reduce(r, v, AX, ALU.add))
                link(V.reciprocal(r, r))
                V.tensor_tensor(v, v, over(r, M), ALU.mult).then_inc(sem("n_p2", s), 1)

            for half in range(2):
                kernel1(s, half)
                kernels23(s, half)
                if half:
                    normalise(s, 0)
                yield f"n.s{half}"
            normalise(s, 1)
            yield "n.col0"
            dve.wait_ge(sem("n_colsum", s), 2)
            link(V.tensor_reduce(sm(s, "rd"), bank(s, 0).rearrange("p (a b) -> p a b", b=M), AX, ALU.max))
            link(V.reciprocal(sm(s, "rd"), sm(s, "rd")))
            V.tensor_scalar(sm(s, "mx2"), sm(s, "rd"), -1.0, None, ALU.mult).then_inc(sem("n_rd", s), 1)
            dve.wait_ge(sem("n_rd", s), 1)
            yield "n.col1"
            yield "n.e3T"
            yield "n.e1T"
            for c in range(2):
                dve.wait_ge(sem("n_kkT", s), c + 1)
                for m in halves:
                    v = PS[s][m, c, 0:4 * M].rearrange("p (a b) -> p a b", b=M)
                    ins = V.tensor_tensor(ey[s][m, c:PAIRS:2, m], v,
                                          sm(s, "mx2")[m, c:PAIRS:2].unsqueeze(2).to_broadcast([M, 4, M]), ALU.mult)
            link(ins)
            for m in halves:
                E = ey[s][m, :, m]
                ins = V.tensor_tensor(E, E, w("ident2")[m].unsqueeze(1).to_broadcast([M, PAIRS, M]), ALU.add)
            ins.then_inc(sem("n_E0", s), 1)
            yield "n.kkT"
            dve.wait_ge(sem("n_y0", s), 1)
            v = bank(s, 2, 0, 128).rearrange("p (a b) -> p a b", b=16)
            link(V.reciprocal(sm(s, "rs3"), v[:, :, HD]))
            V.tensor_tensor(ey[s][:, :, 2 * M:PW], v[:, :, 0:HD], over(sm(s, "rs3"), HD), ALU.mult).then_inc(sem("n_y", s), 1)
            yield "n.y0"
            for k in range(NEWTON):
                for g in range(3):
                    dve.wait_ge(sem("n_S", s), 3 * k + g + 1)
                    ps = pairs_of(s, k, 0, g)[1]
                    Ey, Y = ss[s][:, ps, 2 * M:PW], ey[s][:, ps, 2 * M:PW]
                    V.tensor_tensor(uu[s][:, ps], Ey, Y, ALU.add)
                    ins = V.scalar_tensor_tensor(wz[s][:, ps, 2 * M:PW], Ey, 0.25, Y, ALU.mult, ALU.add)
                    if k < NEWTON - 1:
                        ins = V.scalar_tensor_tensor(wz[s][:, ps, 0:2 * M], ey[s][:, ps, 0:2 * M], 3.0,
                                                     ss[s][:, ps, 0:2 * M], ALU.mult, ALU.add)
                    ins.then_inc(sem("n_wz", s), 1)
                    yield f"n.S{k}{g}"
                for g in range(3):
                    src, ps = pairs_of(s, k, 1, g)
                    Y = ey[s][:, ps, 2 * M:PW]
                    if k < NEWTON - 1:
                        dve.wait_ge(sem("n_e", s), 3 * k + g + 1)
                        ins = V.scalar_tensor_tensor(Y, Y, 4.0, uu[s][:, ps], ALU.mult, ALU.add)
                    else:
                        dve.wait_ge(sem("n_SW", s), 3 * k + g + 1)
                        ins = V.tensor_tensor(Y, src[:, :, 2 * M:PW], uu[s][:, ps], ALU.add)
                    ins.then_inc(sem("n_y", s), 1)
                    yield f"n.W{k}{g}"
            dve.wait_ge(sem("n_w_ps", s), 1)
            V.tensor_tensor(w9[s][:, :, 0:HD], bank(s, 0, 0, 128).rearrange("p (a b) -> p a b", b=16)[:, :, 0:HD],
                            over(sm(s, "rd"), HD), ALU.mult).then_inc(sem("n_w9", s), 1)
            yield "n.w"
            yield "n.o"
            tail(s, 1)
            yield "n.rows"
            yield "n.z"
            ln_stats(s, 1, xin[s][:])
            stats(s, res[s][:], "st", "mv", "ve").then_inc(sem("ln_ve", s), 1)
            yield "n.out"
            dve.wait_ge(stored[s], first * (16 // LANES) + 16)
            ln_rows(s, 1, 1)
            yield "n.ln"

        def beside(s, n_att, half):
            b = 1 + 2 * half
            if n_att == 1:
                dve.wait_ge(sem("y_qk_ps", s), half + 1)
                V.tensor_tensor(k8[s][:, 4 * half:4 * half + 4], bank(s, b).rearrange("p (a b) -> p a b", a=4),
                                over(w("y_bk", 4 * half, 4), 128), ALU.add).then_inc(sem("y_qk", s), 1)
            else:
                dve.wait_ge(sem("y_v_ps", s), half + 1)
                V.tensor_tensor(v8[s][:, half], bank(s, b), row("y_bv")[:, 512 * half:512 * half + 512], ALU.add
                                ).then_inc(sem("y_v8", s), 1)

        def attention8(s, n_att, aug, residual, n_ln):
            if aug:
                dve.wait_ge(sem("a_proj", s), 1)
                V.tensor_tensor(q4[s][:], bank(s, 0).rearrange("p (g t) -> p g t", g=TG), every(w("qaug"), TG),
                                ALU.add).then_inc(sem("a_q", s), 1)
                dve.wait_ge(sem("a_proj", s), 2)
                V.tensor_tensor(k4[s][:], bank(s, 1).rearrange("p (g t) -> p g t", g=TG),
                                o["kaug"][:], ALU.add).then_inc(sem("a_k4", s), 1)
            else:
                dve.wait_ge(sem("a_proj", s), 3 * (n_att - 1) + 2)
                V.tensor_tensor(k4[s][:], every(bank(s, 1, 0, 128), TJ), over(w("hmask"), 128), ALU.mult
                                ).then_inc(sem("a_k4", s), 1)
            dve.wait_ge(sem("a_k4", s), n_att)
            for g in range(2):
                V.tensor_scalar(k_alone(s, g), k4[s][:], w("gmask", g, 1), None, ALU.mult).then_inc(sem("a_k01", s), 1)
            dve.wait_ge(sem("a_proj", s), 3 * n_att)
            V.tensor_copy(v9[s][:, :, 0:HD], bank(s, 2, 0, D).rearrange("p (h e) -> p h e", e=HD)).then_inc(sem("a_v9", s), 1)

            def mx(s, g):
                dve.wait_ge(sem("a_s", s), 4 * (n_att - 1) + g + 1)
                link(V.tensor_reduce(sm(s, "mx", 4 * g, 4), bank(s, g % 2).rearrange("p (a b) -> p a b", a=4), AX, ALU.max))
                V.tensor_scalar(sm(s, "nb", 4 * g, 4), sm(s, "mx", 4 * g, 4), -SC8, None, ALU.mult).then_inc(sem("a_nb", s), 1)

            yield f"r{n_att}.proj"
            mx(s, 0)
            mx(s, 1)
            yield f"r{n_att}.first"
            for g in range(TG):
                yield f"r{n_att}.s{g}"
                n = 4 * (n_att - 1) + g
                dve.wait_ge(sem("a_pT_ps", s), n + 1)
                if g >= 2:
                    dve.wait_ge(sem("a_pv", s), n - 1)
                V.tensor_copy(pT[s][g % 2][:].rearrange("p a b -> p (a b)"), bank(s, 2)).then_inc(sem("a_pT", s), 1)
                if g == 1:
                    mx(s, 2)
                    mx(s, 3)
                if g == 3 and n_att == 1:
                    dve.wait_ge(sem("ctx_in", s), 48)
                    stats(s, cs[s][:], "cst", "cmv", "cve").then_inc(sem("y_cve", s), 1)
                    V.tensor_scalar(madd[s][:], ms[s][:], 0.0, NEG, ALU.is_equal, ALU.mult).then_inc(sem("y_mask", s), 1)
                yield f"r{n_att}.t{g}"
            if n_att == 1:
                dve.wait_ge(sem("y_crstd", s), 1)
                V.tensor_scalar(cn[s][:], cs[s][:], sm(s, "cmv", 0, 1), sm(s, "crstd"), ALU.subtract, ALU.mult
                                ).then_inc(sem("y_cn", s), 1)
            yield f"r{n_att}.last"
            tail(s, 1 + n_att)
            if n_att == 1:
                dve.wait_ge(sem("y_cnT_ps", s), 1)
                V.tensor_scalar(cnT[s][:], bank(s, 1, 0, 128), w("y_g"), w("y_b"), ALU.mult, ALU.add).then_inc(sem("y_T", s), 1)
            yield f"r{n_att}.rows"
            yield f"r{n_att}.z"
            ln_stats(s, n_ln - (n_ln > 3), residual(s))
            stats(s, res[s][:], "st", "mv", "ve").then_inc(sem("ln_ve", s), 1)
            beside(s, n_att, 0)
            yield f"r{n_att}.out"
            ln_rows(s, n_ln, n_ln)
            beside(s, n_att, 1)
            yield f"r.ln{n_ln}"

        def rest(s):
            yield from attention8(s, 1, True, lambda s: xs[s][:], 2)

            dve.wait_ge(sem("m_logits", s), 1)
            link(V.tensor_tensor(sm(s, "lg"), bank(s, 3, 0, EXPERTS), row("m_br"), ALU.add))
            link(V.tensor_reduce(sm(s, "pmx"), sm(s, "lg"), AX, ALU.max))
            V.tensor_scalar(sm(s, "pnb"), sm(s, "pmx"), -1.0, None, ALU.mult).then_inc(sem("m_pnb", s), 1)
            yield "rm.first"
            dve.wait_ge(sem("m_e8", s), 1)
            link(V.tensor_reduce(sm(s, "emx"), sm(s, "e8"), AX, ALU.max))
            V.reciprocal(sm(s, "grs"), sm(s, "psum"))
            link(V.tensor_scalar(sm(s, "gate"), sm(s, "e8"), sm(s, "emx"), None, ALU.is_ge))
            link(V.tensor_tensor(sm(s, "gate"), sm(s, "gate"), w("first"), ALU.mult))
            link(V.tensor_reduce(sm(s, "fmx"), sm(s, "gate"), AX, ALU.max))
            link(V.tensor_tensor(sm(s, "gp"), sm(s, "emx"), sm(s, "grs"), ALU.mult))
            V.tensor_scalar(sm(s, "gate"), sm(s, "gate"), sm(s, "fmx"), sm(s, "gp"), ALU.is_ge, ALU.mult
                            ).then_inc(sem("m_gate", s), 1)

            def relu(s, t):
                dve.wait_ge(sem("m_h_ps", s), t + 1)
                if t >= 2:
                    dve.wait_ge(sem("m_y", s), t - 1)
                for c in range(4):
                    ins = V.tensor_scalar(hT[s][t % 2][:, c], bank(s, t % 2, 128 * c, 128), w("m_b1", 4 * t + c, 1), 0.0,
                                          ALU.add, ALU.max)
                ins.then_inc(sem("m_h1", s), 1)

            for t in range(4):
                if t % 2 == 0:
                    relu(s, t + 1)
                yield f"rm.h{t}"
                if t == 0:
                    dve.wait_ge(sem("m_b2", s), 1)
                    V.tensor_tensor(res[s][:], bank(s, 3, 256, D), xs[s][:], ALU.add).then_inc(sem("m_res", s), 1)
                    dve.wait_ge(sem("m_res", s), 1)
                dve.wait_ge(sem("m_y", s), t + 1)
                for e in (2 * t, 2 * t + 1):
                    V.scalar_tensor_tensor(res[s][:], bank(s, 2 + t % 2, 128 * (e % 2), 128), sm(s, "gate", e, 1), res[s][:],
                                           ALU.mult, ALU.add).then_inc(sem("m_y_used", s), 1)
                    dve.wait_ge(sem("m_y_used", s), e + 1)
                if t == 3:
                    stats(s, res[s][:], "st", "mv", "ve").then_inc(sem("ln_ve", s), 1)
                yield f"rm.y{t}"
            ln_rows(s, 3, 3)
            yield "r.ln3"

            def xbo_of(s):
                dve.wait_ge(sem("xbo", s), 1)
                return xbo[s][:]

            yield from attention8(s, 2, False, xbo_of, 4)

            dve.wait_ge(sem("ln_rows", s), 4)
            stats(s, xs[s][:], "st", "mv", "ve").then_inc(sem("ln_ve", s), 1)
            yield "ry.stats"
            dve.wait_ge(sem("ln_rstd", s), 5)
            V.tensor_scalar(xn[s][:], xs[s][:], sm(s, "mv", 0, 1), sm(s, "rstd"), ALU.subtract, ALU.mult
                            ).then_inc(sem("y_xn", s), 1)
            yield "ry.norm"
            dve.wait_ge(sem("y_xnT_ps", s), 1)
            V.tensor_scalar(xnT[s][:], bank(s, 1, 128, 128), w("y_g"), w("y_b"), ALU.mult, ALU.add).then_inc(sem("y_T", s), 1)
            yield "ry.T"
            for b in range(2):
                dve.wait_ge(sem("y_qk_ps", s), b + 3)
                V.tensor_tensor(q8[s][:, 4 * b:4 * b + 4], bank(s, b).rearrange("p (a b) -> p a b", a=4),
                                over(w("y_bq", 4 * b, 4), 128), ALU.add).then_inc(sem("y_qk", s), 1)
                yield f"ry.q{b}"

            def ymax(s, g):
                dve.wait_ge(sem("y_s", s), g + 1)
                link(V.tensor_reduce(sm(s, "mx", 4 * g, 4), bank(s, g % 2).rearrange("p (a b) -> p a b", a=4), AX, ALU.max))
                V.tensor_scalar(sm(s, "nb", 4 * g, 4), sm(s, "mx", 4 * g, 4), -SC64, None, ALU.mult).then_inc(sem("y_nb", s), 1)

            ymax(s, 0)
            ymax(s, 1)
            yield "ry.first"
            for g in range(4):
                dve.wait_ge(sem("y_e", s), g + 1)
                r = sm(s, "rs", 4 * g, 4)
                V.reciprocal(r, r).then_inc(sem("y_rs", s), 1)
                dve.wait_ge(sem("y_rs", s), g + 1)
                v = pe_[s][g % 2][:, 2:4]
                V.tensor_tensor(v, v, over(r[:, 2:4], 128), ALU.mult).then_inc(sem("y_p", s), 1)
                yield f"ry.s{g}"
                dve.wait_ge(sem("y_pT_ps", s), g + 1)
                if g >= 2:
                    dve.wait_ge(sem("y_pv", s), g - 1)
                V.tensor_copy(pT[s][g % 2][:].rearrange("p a b -> p (a b)"), bank(s, 2)).then_inc(sem("y_pT", s), 1)
                if g == 1:
                    ymax(s, 2)
                    ymax(s, 3)
                yield f"ry.t{g}"
            yield "ry.last"
            dve.wait_ge(sem("xbo", s), 2)
            ln_stats(s, 4, xbo[s][:])
            stats(s, res[s][:], "st", "mv", "ve").then_inc(sem("ln_ve", s), 1)
            yield "ry.out"
            ln_rows(s, 5, 6)
            yield "r.ln5"

            dve.wait_ge(sem("f_h", s), 1)
            h, u = hT[s][0][:], hT[s][1][:]
            V.scalar_tensor_tensor(u, u, 1.0, h, ALU.add, ALU.mult).then_inc(sem("f_u", s), 1)
            yield "rf.h"
            dve.wait_ge(sem("f_t", s), 1)
            V.scalar_tensor_tensor(u, u, 1.0, h, ALU.add, ALU.mult).then_inc(sem("f_g", s), 1)
            yield "rf.u"
            ln_stats(s, 5, xs[s][:])
            stats(s, res[s][:], "st", "mv", "ve").then_inc(sem("ln_ve", s), 1)
            yield "rf.out"
            ln_rows(s, 6, 7)
            yield "rf.ln"

        run(nystrom, rest)


def y_o8(nc, act, sem, s, g, o8, PS):
    act.wait_ge(sem("y_pv", s), g + 1)
    h = y_head(g, 0)
    nc.scalar.copy(o8[s][:].rearrange("p a (b c) -> p (a b) c", c=M)[:, h:h + 7:2],
                   PS[s][:, 3, 256 * (g % 2):256 * (g % 2) + 256].rearrange("p (a b) -> p a b", a=4)
                   ).then_inc(sem("y_o8", s), 1)


def y_head(g, j):
    return 2 * (4 * (g // 2) + j) + g % 2


def kernel(**inputs):
    import concourse.bacc as bacc
    from concourse.bass_utils import run_bass_kernel_spmd

    a = {k: np.asarray(v) for k, v in inputs.items()}

    def tiles4(m):
        t = np.zeros((D, TJ, TG, TW), m.dtype)
        t[:, :, :, :HD] = m.reshape(D, TG, TJ, HD).transpose(0, 2, 1, 3)
        return t.reshape(D, H * TW)

    qkv = a["L0_attn_w_qkv"]
    kv = a["L0_xattn_w_kv"]
    part = {
        "n_q": qkv[:, :D], "n_k": qkv[:, D:2 * D], "n_v": qkv[:, 2 * D:], "n_p": a["L0_attn_w_proj"],
        "x_q4": tiles4(a["L0_xattn_w_q"]), "x_k4": tiles4(kv[:, :D]), "x_v": kv[:, D:], "x_p": a["L0_xattn_w_proj"],
        "c_q": a["L1_attn_Wq"].T, "c_k": a["L1_attn_Wk"].T, "c_v": a["L1_attn_Wv"].T,
        "c_p": a["L1_attn_Wo"].T,
        "m_r": a["L0_ffn_Wr"], "m_1": a["L0_ffn_W1"].transpose(1, 0, 2).reshape(D, -1),
        "m_2": a["L0_ffn_W2"].reshape(16, 128, D).transpose(1, 0, 2).reshape(128, -1),
        "y_q": a["L1_xattn_Wq"], "y_k": a["L1_xattn_Wk"], "y_v": a["L1_xattn_Wv"],
        "y_p": a["L1_xattn_Wo"].reshape(8, 128, D).transpose(1, 0, 2).reshape(128, -1),
        "m_b1": a["L0_ffn_b1"].reshape(16, 128).T, "y_bq": a["L1_xattn_bq"].reshape(8, 128).T,
        "y_bk": a["L1_xattn_bk"].reshape(8, 128).T, "y_g": a["L1_xattn_gamma"][:, None],
        "y_b": a["L1_xattn_beta"][:, None],
        "x_rel": np.repeat(a["L0_xattn_w_rel"].reshape(TG, TJ), TW, axis=0),
    }
    f = np.float32
    part["ident"] = np.eye(128, dtype=f)
    part["ones2"] = np.kron(np.eye(2, dtype=f), np.ones((M, M), f))
    part["ident2"] = np.tile(np.eye(M, dtype=f), (2, 1))
    pos, at = np.arange(128, dtype=f), np.arange(128) % TW
    part["qaug"] = np.where(at[:, None] == HD, pos[None], np.where(at[:, None] == HD + 1, -1, 0)).astype(f)
    part["kpat"] = ((at == HD) | (at == HD + 1)).astype(f)[:, None] * np.ones((1, 128), f)
    part["kpos"] = np.where(at[:, None] == HD + 1, pos[None], 1).astype(f)
    part["causal"] = np.triu(np.full((128, 128), -1e30, f), 1)
    part["first"] = np.tile(EXPERTS - np.arange(EXPERTS, dtype=f), (128, 1))
    part["mask16"] = (np.arange(128)[:, None] // TW * TJ + np.arange(128)[:, None] % TW // HD == np.arange(H)).astype(f)
    part["hmask"] = (np.arange(128)[:, None] % TW // HD == np.arange(TJ)).astype(f)
    part["mhalf"] = np.full((128, 1), -0.5, f)
    part["gmask"] = (np.arange(128)[:, None] // TW == np.arange(TG)).astype(f)
    wpack = np.concatenate([part[n] for n, _ in WEIGHTS], axis=1)
    rows = np.concatenate([a["L0_ffn_br"], a["L1_attn_bo"], a["L1_xattn_bo"], a["L1_xattn_bv"],
                           a["L1_ffn_fc1_logits"], a["L1_ffn_fc2_logits"]])[None]

    def chunks(m):
        return m.reshape(16, 128, -1).transpose(1, 0, 2)

    arrays = {
        "x": a["x"], "xT": a["x"].transpose(0, 2, 1), "ctx": a["ctx_1024"], "ctxT": a["ctx_1024"].transpose(0, 2, 1),
        "mask": a["mask_Bx1xSxS2_ik1"].reshape(B, S, S), "wpack": wpack, "rows": rows, "b2": a["L0_ffn_b2"],
        "a1": chunks(a["L1_ffn_fc1_A"].transpose(0, 2, 1)), "b1": chunks(a["L1_ffn_fc1_B"]),
        "a2": chunks(a["L1_ffn_fc2_A"].transpose(0, 2, 1)), "b2w": chunks(a["L1_ffn_fc2_B"]),
    }
    arrays = {f"in_{k}": np.ascontiguousarray(v) for k, v in arrays.items()}
    nc = bacc.Bacc("TRN2", target_bir_lowering=False, num_devices=1)
    args = [nc.dram_tensor(k, v.shape, mybir.dt.from_np(v.dtype), kind="ExternalInput").ap() for k, v in arrays.items()]
    out = nc.dram_tensor("out", (B, S, D), F32, kind="ExternalOutput").ap()
    build(nc, *args, out)
    r = run_bass_kernel_spmd(nc, [arrays], core_ids=[0])
    return r.results[0]["out"]
```
